# Optimizing a Trainium2 kernel written in Bass

```python
import numpy as np
import jax
import jax.numpy as jnp

def _softmax(x, axis=-1):
    return jax.nn.softmax(x, axis=axis)

def _gelu(x):
    return jax.nn.gelu(x, approximate=True)

def _silu(x):
    return jax.nn.silu(x)

def _sigmoid(x):
    return jax.nn.sigmoid(x)

def _layernorm(x, axis=-1, eps=1e-05):
    m = jnp.mean(x, axis=axis, keepdims=True)
    v = jnp.var(x, axis=axis, keepdims=True)
    return (x - m) / jnp.sqrt(v + eps)

def _scatter_add(tgt, idx, src, axis=0):
    return tgt.at[idx].add(src)

def _segment_sum(src, seg, n):
    return jax.ops.segment_sum(src, seg, n)
kernel_name = 'mk_adj_resnorm_d1_adj_r2_8d99d3'

def setup_inputs(seed: int=0):
    np.random.seed(seed)
    _w = jnp.asarray

    def _rec_inputs():
        import jax
        import jax.numpy as jnp
        _gk = jax.random.key(seed)
        x = -0.0005207 + 1.001 * jax.random.normal(jax.random.fold_in(_gk, 1), (2048, 256), jnp.float32)
        _a = jax.random.bernoulli(jax.random.fold_in(_gk, 2), 0.00195312, (2048, 2048))
        adj = _a.astype(jnp.int32)
        _nm = jnp.ones((2048,), dtype=bool)
        nodemask = jnp.where(_nm, 1.0, 0.0).astype(jnp.int32)
        return (x, adj, nodemask)
    x, adj, nodemask = _rec_inputs()

    def _L0_gnn_setup():
        import jax, jax.numpy as jnp
        import numpy as np
        D = 256
        H = 8
        HD = D // H
        EPS = 1e-05
        NEG = -1e+30

        def layer_norm(x, scale, bias):
            mu = jnp.mean(x, axis=-1, keepdims=True)
            var = jnp.mean(jnp.square(x - mu), axis=-1, keepdims=True)
            return (x - mu) * jax.lax.rsqrt(var + EPS) * scale + bias
        key = jax.random.key(seed)
        ks = jax.random.split(key, 16)
        S = T = 2048
        inp = {'h_source': jax.random.normal(ks[0], (S, D), jnp.float32), 'h_target': jax.random.normal(ks[1], (T, D), jnp.float32), 'edge_mask': jax.random.randint(ks[2], (T, S), 0, 2, jnp.int32), 'source_mask': jnp.ones((S,), jnp.int32), 'target_mask': jnp.ones((T,), jnp.int32), 'ln1_scale': jnp.ones((D,), jnp.float32), 'ln1_bias': jnp.zeros((D,), jnp.float32), 'Wq': jax.random.normal(ks[3], (D, D), jnp.float32) / np.sqrt(D), 'bq': jnp.zeros((D,), jnp.float32), 'Wk': jax.random.normal(ks[4], (D, D), jnp.float32) / np.sqrt(D), 'bk': jnp.zeros((D,), jnp.float32), 'Wv': jax.random.normal(ks[5], (D, D), jnp.float32) / np.sqrt(D), 'bv': jnp.zeros((D,), jnp.float32), 'Wo': jax.random.normal(ks[6], (D, D), jnp.float32) / np.sqrt(D), 'bo': jnp.zeros((D,), jnp.float32), 'ln2_scale': jnp.ones((D,), jnp.float32), 'ln2_bias': jnp.zeros((D,), jnp.float32), 'W1': jax.random.normal(ks[7], (D, 4 * D), jnp.float32) / np.sqrt(D), 'W2': jax.random.normal(ks[8], (4 * D, D), jnp.float32) / np.sqrt(4 * D)}
        return inp
    _L0_gnn_all = _L0_gnn_setup()
    _L0_gnn_in = {k: v for k, v in _L0_gnn_all.items() if k in ('h_target', 'ln1_scale', 'ln1_bias', 'Wq', 'bq', 'Wk', 'bk', 'Wv', 'bv', 'Wo', 'bo', 'ln2_scale', 'ln2_bias', 'W1', 'W2')}
    del _L0_gnn_all
    return {'x': x, 'adj': adj, 'nodemask': nodemask, 'L0_gnn_h_target': _L0_gnn_in['h_target'], 'L0_gnn_ln1_scale': _L0_gnn_in['ln1_scale'], 'L0_gnn_ln1_bias': _L0_gnn_in['ln1_bias'], 'L0_gnn_Wq': _L0_gnn_in['Wq'], 'L0_gnn_bq': _L0_gnn_in['bq'], 'L0_gnn_Wk': _L0_gnn_in['Wk'], 'L0_gnn_bk': _L0_gnn_in['bk'], 'L0_gnn_Wv': _L0_gnn_in['Wv'], 'L0_gnn_bv': _L0_gnn_in['bv'], 'L0_gnn_Wo': _L0_gnn_in['Wo'], 'L0_gnn_bo': _L0_gnn_in['bo'], 'L0_gnn_ln2_scale': _L0_gnn_in['ln2_scale'], 'L0_gnn_ln2_bias': _L0_gnn_in['ln2_bias'], 'L0_gnn_W1': _L0_gnn_in['W1'], 'L0_gnn_W2': _L0_gnn_in['W2']}

def reference(x, adj, nodemask, L0_gnn_h_target, L0_gnn_ln1_scale, L0_gnn_ln1_bias, L0_gnn_Wq, L0_gnn_bq, L0_gnn_Wk, L0_gnn_bk, L0_gnn_Wv, L0_gnn_bv, L0_gnn_Wo, L0_gnn_bo, L0_gnn_ln2_scale, L0_gnn_ln2_bias, L0_gnn_W1, L0_gnn_W2):
    import jax
    import jax.numpy as jnp

    def _L0_gnn_ref(h_source, h_target, edge_mask, source_mask, target_mask, ln1_scale, ln1_bias, Wq, bq, Wk, bk, Wv, bv, Wo, bo, ln2_scale, ln2_bias, W1, W2):
        import jax, jax.numpy as jnp
        import numpy as np
        D = 256
        H = 8
        HD = D // H
        EPS = 1e-05
        NEG = -1e+30

        def layer_norm(x, scale, bias):
            mu = jnp.mean(x, axis=-1, keepdims=True)
            var = jnp.mean(jnp.square(x - mu), axis=-1, keepdims=True)
            return (x - mu) * jax.lax.rsqrt(var + EPS) * scale + bias
        smask = (source_mask == 1)[:, None]
        tmask = (target_mask == 1)[:, None]
        hs = layer_norm(h_source, ln1_scale, ln1_bias)
        ht = layer_norm(h_target, ln1_scale, ln1_bias)
        hs = jnp.where(smask, hs, 0.0)
        ht = jnp.where(tmask, ht, 0.0)
        T, S = (ht.shape[0], hs.shape[0])
        q = (ht @ Wq + bq).reshape(T, H, HD) / jnp.sqrt(jnp.float32(HD))
        k = (hs @ Wk + bk).reshape(S, H, HD)
        v = (hs @ Wv + bv).reshape(S, H, HD)
        logits = jnp.einsum('thd,shd->hts', q, k)
        logits = jnp.where(edge_mask[None] != 0, logits, NEG)
        probs = jax.nn.softmax(logits, axis=-1)
        ctx = jnp.einsum('hts,shd->thd', probs, v).reshape(T, D)
        attn = ctx @ Wo + bo
        attn = jnp.where(tmask, attn, 0.0)
        ht = ht + attn
        ht = layer_norm(ht, ln2_scale, ln2_bias)
        ht = jnp.where(tmask, ht, 0.0)
        ff = jax.nn.gelu(ht @ W1) @ W2
        return ht + ff
    x = _layernorm(x + _L0_gnn_ref(x, L0_gnn_h_target, adj, nodemask, nodemask, L0_gnn_ln1_scale, L0_gnn_ln1_bias, L0_gnn_Wq, L0_gnn_bq, L0_gnn_Wk, L0_gnn_bk, L0_gnn_Wv, L0_gnn_bv, L0_gnn_Wo, L0_gnn_bo, L0_gnn_ln2_scale, L0_gnn_ln2_bias, L0_gnn_W1, L0_gnn_W2), axis=-1)
    return x

_drawn_inputs = setup_inputs


def setup_inputs(seed=0):
    import zlib

    import numpy as np

    out = dict(_drawn_inputs(seed))
    spreads = {'L0_gnn_ln1_scale': (1.0, 0.2),
     'L0_gnn_ln1_bias': (0.0, 0.1),
     'L0_gnn_bq': (0.0, 0.415),
     'L0_gnn_bk': (0.0, 0.8),
     'L0_gnn_bv': (0.0, 0.1),
     'L0_gnn_bo': (0.0, 0.1),
     'L0_gnn_ln2_scale': (1.0, 0.2),
     'L0_gnn_ln2_bias': (0.0, 0.1)}
    factors = {}
    for name, (base, spread) in spreads.items():
        noise = np.random.default_rng([zlib.crc32(name.encode()), seed]).standard_normal(out[name].shape)
        drawn = base * np.exp(spread * noise) if base else spread * noise
        out[name] = jnp.asarray(drawn.astype(out[name].dtype))
    for name, factor in factors.items():
        out[name] = (out[name] * factor).astype(out[name].dtype)
    return out
```

```python
from contextlib import ExitStack

import concourse.bass as bass
from concourse import mybir

ALU = mybir.AluOpType
ACT = mybir.ActivationFunctionType
AX = mybir.AxisListType
F32 = mybir.dt.float32
F32R = mybir.dt.float32r
BF16 = mybir.dt.bfloat16
I32 = mybir.dt.int32

P = 128
EPS = 1e-5
NEG = -1e30
LOWEST = -3.0e38
ds = bass.ds


def graph_attention(nc, x, adj, nodemask, h_target, ln1_scale, ln1_bias, Wq, bq, Wk, bk, Wv, bv, Wo, bo,
                    ln2_scale, ln2_bias, W1, W2, out):
    N, D = x.shape
    H = 8
    HD = D // H
    DF = W1.shape[1]
    TILES = N // P
    DK = D // P
    FK = DF // P
    CH = 512
    CT = CH // P
    CHUNKS = N // CH
    HALF = N // 2
    HPG = 4
    GROUPS = H // HPG
    QUARTERS = 4
    LR = 4
    Q_SCALE = 1.0 / float(HD) ** 0.5
    STACK = 3 * HD

    ctx = ExitStack()
    with ctx:
        def sb(name, shape, dt=F32):
            return ctx.enter_context(nc.sbuf_tensor(name, shape, dt))

        def sem(name):
            return ctx.enter_context(nc.semaphore(name))

        ht_dram = nc.dram_tensor("ht_scratch", (N, D), F32).ap()
        ctx_dram = nc.dram_tensor("ctx_scratch", (N, D), F32).ap()

        k_stack = sb("k_stack", [STACK, H, N], F32R)
        q_stack = sb("q_stack", [STACK, H, P], F32R)
        q_hi = sb("q_hi", [P, DK, N], F32R)
        q_lo = sb("q_lo", [P, DK, N], F32R)
        v_all = sb("v_all", [P, TILES, D])
        adj_sb = sb("adj_sb", [P, N], I32)
        mask_sb = sb("mask_sb", [P, N], BF16)
        ident = sb("ident", [P, P])
        node = sb("node", [P, TILES])
        node_i = sb("node_i", [P, TILES], I32)
        stats = sb("stats", [P, 2, CT, 6])
        moments = sb("moments", [P, 2, CT, 2])
        var_eps = sb("var_eps", [P, 2, CT])
        rstd = sb("rstd", [P, 2, CT])
        minus_half = sb("minus_half", [P, CT])
        rowmax = sb("rowmax", [P, H, 2])
        negmax = sb("negmax", [P, H])
        sums = sb("sums", [P, H])
        recip = sb("recip", [P, HPG])
        ctx_part = sb("ctx_part", [P, HPG * P])
        ctx_sum = sb("ctx_sum", [P, HPG, HD])
        ctx_norm = sb("ctx_norm", [P, D])

        logits = sb("logits", [P, LR, N])
        probs_t = sb("probs_t", [P, 2, TILES, P])
        k_hi = sb("k_hi", [P, DK, CH], F32R)
        k_lo = sb("k_lo", [P, DK, CH], F32R)
        h_tok = logits[:, 0, :].rearrange("p (s c d) -> p s c d", s=2, c=CT)
        h_feat = logits[:, 1, :].rearrange("p (s k n) -> p s k n", s=2, k=DK)
        raw = logits[:, 2, 0:2 * DK * CH].rearrange("p (s k n) -> p s k n", s=2, k=DK)
        wqkv = logits[:, 3, 0:3 * DK * D].rearrange("p (w k n) -> p w k n", w=3, k=DK)
        ln1_bc = logits[:, 3, 3 * DK * D:3 * DK * D + 2 * D].rearrange("p (w n) -> p w n", w=2)
        bv_bc = probs_t[:, 0, 0:2, :].rearrange("p a b -> p (a b)")
        bqk = probs_t[:, 0, 2, 0:2 * DK].rearrange("p (w k) -> p w k", w=2)
        w1_sb = logits[:, 0, :].rearrange("p (k n) -> p k n", k=DK)
        w2_sb = logits[:, 1, :].rearrange("p (k n) -> p k n", k=FK)
        wo_sb = logits[:, 2, 0:DK * D].rearrange("p (k n) -> p k n", k=DK)
        bo_bc = logits[:, 2, 2 * D:3 * D]
        scale2_bc = logits[:, 2, 3 * D:4 * D]
        bias2_bc = logits[:, 2, 4 * D:5 * D]
        gelu_t = probs_t[:, 0, 0:FK, :]
        ctx_t = probs_t[:, 0, FK:FK + DK, :]
        h2_t = probs_t[:, 0, FK + DK:FK + 2 * DK, :]
        in3 = logits[:, 3, 0:6 * D].rearrange("p (r w n) -> p r w n", r=2, w=3)
        h2 = logits[:, 3, 6 * D:8 * D].rearrange("p (r n) -> p r n", r=2)
        res = probs_t[:, 1, 0:2, :].rearrange("p a b -> p (a b)")
        res2 = probs_t[:, 1, 2:4, :].rearrange("p a b -> p (a b)")
        y_out = probs_t[:, 1, 4:8, :].rearrange("p (r a) b -> p r (a b)", r=2)

        bank = [ctx.enter_context(nc.psum_tensor(f"bank{i}", [P, CH], F32)) for i in range(4)]
        score = [ctx.enter_context(nc.psum_tensor(f"score{i}", [P, HALF], F32)) for i in range(2)]
        turned = bank[0:2]
        ctx_ps = bank[2]
        back_ps = bank[3]

        def dram_tiles(a):
            return a.rearrange("(c t p) d -> p c t d", p=P, t=CT)

        weights_loaded = sem("weights_loaded")
        x_loaded = [sem(f"x_loaded{s}") for s in range(2)]
        zeroed = sem("zeroed")
        ident_ready = sem("ident_ready")
        node_ready = sem("node_ready")
        half_ready = sem("half_ready")
        stat_step = sem("stat_step")
        var_ready = sem("var_ready")
        rstd_ready = sem("rstd_ready")
        norm_step = sem("norm_step")
        ln1_done = sem("ln1_done")
        ht_saved = sem("ht_saved")
        h_turned = sem("h_turned")
        h_copied = sem("h_copied")
        projected = sem("projected")
        v_projected = sem("v_projected")
        raw_ready = sem("raw_ready")
        hi_ready = sem("hi_ready")
        lo_ready = sem("lo_ready")
        v_stored = sem("v_stored")
        k_stacked = sem("k_stacked")
        adj_loaded = sem("adj_loaded")
        mask_ready = sem("mask_ready")
        q_stacked = [sem(f"q_stacked{g}") for g in range(GROUPS)]
        scores_ready = sem("scores_ready")
        masked = sem("masked")
        negmax_ready = sem("negmax_ready")
        probs_ready = sem("probs_ready")
        quarter_turned = sem("quarter_turned")
        copied_act = sem("copied_act")
        copied_dve = sem("copied_dve")
        ctx_done = sem("ctx_done")
        ctx_copied = sem("ctx_copied")
        ctx_back = sem("ctx_back")
        ctx_step = sem("ctx_step")
        ctx_ready = sem("ctx_ready")
        ctx_saved = sem("ctx_saved")
        lone_waits = {eng.engine: sem(f"lone_waits_{n}") for n, eng in (("sp", nc.sync), ("dve", nc.vector))}
        weights3_loaded = sem("weights3_loaded")
        rows_loaded = [sem(f"rows_loaded{r}") for r in range(2)]
        ctxt_turned = sem("ctxt_turned")
        ctxt_copied = sem("ctxt_copied")
        attn_ready = sem("attn_ready")
        ln2_step = sem("ln2_step")
        rstd2_ready = sem("rstd2_ready")
        rstd3_ready = sem("rstd3_ready")
        h2_turned = sem("h2_turned")
        h2_copied = sem("h2_copied")
        hidden_ready = sem("hidden_ready")
        gelu_ready = sem("gelu_ready")
        ff_ready = sem("ff_ready")
        ln3_step = sem("ln3_step")
        y_saved = [sem(f"y_saved{r}") for r in range(2)]

        block = ctx.enter_context(nc.Block())
        UNITS = TILES * H
        N_WEIGHTS = 9
        N_WEIGHTS3 = 6
        STACK_DMAS = 3 * HPG

        def wait_alone(eng, semaphore, value):
            eng.wait_ge(semaphore, value)
            eng.sem_inc(lone_waits[eng.engine], 1)

        @block.sync
        def _(sp):
            sp.dma_start(node_i[:, :], nodemask.rearrange("(t p) -> p t", p=P), allow_slow_non_contiguous=True).then_inc(weights_loaded, 16)
            sp.dma_start(ln1_bc[:, 0, :], ln1_scale.partition_broadcast(P)).then_inc(weights_loaded, 16)
            sp.dma_start(ln1_bc[:, 1, :], ln1_bias.partition_broadcast(P)).then_inc(weights_loaded, 16)

            def load_x(s, c):
                src = dram_tiles(x if s == 0 else h_target)
                sp.dma_start(h_tok[:, s, :, :], src[:, c, :, :]).then_inc(x_loaded[s], 16)

            load_x(0, 0)
            load_x(1, 0)
            for w, a in enumerate((Wk, Wv, Wq)):
                sp.dma_start(wqkv[:, w, :, :], a.rearrange("(k p) n -> p k n", p=P)).then_inc(weights_loaded, 16)
            sp.dma_start(bv_bc, bv.partition_broadcast(P)).then_inc(weights_loaded, 16)
            for w, a in enumerate((bk, bq)):
                sp.dma_start(bqk[:, w, :], a.rearrange("(k p) -> p k", p=P), allow_slow_non_contiguous=True).then_inc(weights_loaded, 16)
            sp.dma_start(adj_sb[:, :], adj[0:P, :]).then_inc(adj_loaded, 16)

            def prepare(c, last):
                wait_alone(sp, ln1_done, 2 * CT * c + 2 * CT)
                sp.dma_start(dram_tiles(ht_dram)[:, c, :, :], h_tok[:, 1, :, :]).then_inc(ht_saved, 16)
                if not last:
                    for s in range(2):
                        wait_alone(sp, h_turned, 2 * c + s + 1)
                        if s == 1:
                            wait_alone(sp, ht_saved, 16 * (c + 1))
                        load_x(s, c + 1)
                wait_alone(sp, lo_ready, 2 * c + 1)
                for g, part in enumerate((k_hi, k_lo, k_hi)):
                    for q in range(HPG):
                        dst = k_stack[HD * g:HD * (g + 1), :, ds(c * CH, CH)].rearrange(
                            "p (k q) n -> p q k n", q=HPG)[:, q, :, :]
                        sp.dma_start(dst.bitcast(F32), part[HD * q:HD * (q + 1), :, :].bitcast(F32)).then_inc(k_stacked, 16)

            with sp.Fori(0, CHUNKS - 1) as c:
                prepare(c, False)
            prepare(CHUNKS - 1, True)

            def stack_q(t, g):
                for r, part in enumerate((q_hi, q_hi, q_lo)):
                    for q in range(HPG):
                        sp.dma_start(q_stack[HD * r:HD * (r + 1), g * HPG + q, :].bitcast(F32),
                                     part[HD * q:HD * (q + 1), g, ds(t * P, P)].bitcast(F32)).then_inc(q_stacked[g], 16)

            sp.wait_ge(lo_ready, 2 * CHUNKS)
            for g in range(GROUPS):
                stack_q(0, g)

            def attend(t, last):
                if not last:
                    wait_alone(sp, mask_ready, t + 1)
                    sp.dma_start(adj_sb[:, :], adj[ds((t + 1) * P, P), :]).then_inc(adj_loaded, 16)
                    for g in range(GROUPS):
                        wait_alone(sp, scores_ready, 2 * (t * H + HPG * (g + 1)))
                        stack_q(t + 1, g)
                wait_alone(sp, ctx_ready, GROUPS * (t + 1))
                sp.dma_start(ctx_dram[ds(t * P, P), :], ctx_norm[:, :]).then_inc(ctx_saved, 16)

            with sp.Fori(0, TILES - 1) as t:
                attend(t, False)
            sp.wait_ge(quarter_turned, QUARTERS * UNITS)
            sp.dma_start(w1_sb, W1.rearrange("(k p) n -> p k n", p=P)).then_inc(weights3_loaded, 16)
            sp.dma_start(w2_sb, W2.rearrange("(k p) n -> p k n", p=P)).then_inc(weights3_loaded, 16)
            sp.dma_start(wo_sb, Wo.rearrange("(k p) n -> p k n", p=P)).then_inc(weights3_loaded, 16)
            for dst, a in ((bo_bc, bo), (scale2_bc, ln2_scale), (bias2_bc, ln2_bias)):
                sp.dma_start(dst, a.partition_broadcast(P)).then_inc(weights3_loaded, 16)
            attend(TILES - 1, True)
            sp.wait_ge(ctx_saved, 16 * TILES)
            sp.wait_ge(ht_saved, 16 * CHUNKS)

            def load_rows(t, r):
                for w, a in enumerate((ctx_dram, ht_dram, x)):
                    sp.dma_start(in3[:, r, w, :], a[ds(t * P, P), :]).then_inc(rows_loaded[r], 16)

            def save_rows(t, r):
                wait_alone(sp, ln3_step, 6 * t + 6)
                sp.dma_start(out[ds(t * P, P), :], y_out[:, r, :]).then_inc(y_saved[r], 16)

            load_rows(0, 0)
            load_rows(1, 1)

            def finish(i, last):
                for r in range(2):
                    save_rows(2 * i + r, r)
                    if not last:
                        load_rows(2 * i + 2 + r, r)

            with sp.Fori(0, TILES // 2 - 1) as i:
                finish(i, False)
            finish(TILES // 2 - 1, True)
            for r in range(2):
                sp.wait_ge(y_saved[r], 16 * (TILES // 2))

        @block.gpsimd
        def _(pool):
            pool.memset(ident[:, :], 0.0).then_inc(zeroed, 1)
            pool.wait_ge(zeroed, 1)
            pool.affine_select(out=ident[:, :], in_=ident[:, :], compare_op=ALU.not_equal, fill=1.0, base=0,
                               pattern=[[-1, P]], channel_multiplier=1).then_inc(ident_ready, 1)
            pool.memset(minus_half[:, :], -0.5).then_inc(half_ready, 1)
            pool.wait_ge(half_ready, 1)

            def rsqrt1(c):
                for s in range(2):
                    pool.wait_ge(var_ready, 2 * c + s + 1)
                    pool.tensor_tensor(rstd[:, s, :], var_eps[:, s, :], minus_half[:, :], ALU.pow).then_inc(rstd_ready, 1)

            with pool.Fori(0, CHUNKS) as c:
                rsqrt1(c)

            def rsqrt2(t):
                pool.wait_ge(ln2_step, 8 * t + 5)
                pool.tensor_tensor(rstd[:, 0, 0:1], var_eps[:, 0, 0:1], minus_half[:, 0:1], ALU.pow).then_inc(rstd2_ready, 1)

            def rsqrt3(t):
                pool.wait_ge(ln3_step, 6 * t + 5)
                pool.tensor_tensor(rstd[:, 1, 0:1], var_eps[:, 1, 0:1], minus_half[:, 0:1], ALU.pow).then_inc(rstd3_ready, 1)

            rsqrt2(0)
            with pool.Fori(0, TILES - 1) as t:
                rsqrt2(t + 1)
                rsqrt3(t)
            rsqrt3(TILES - 1)

        @block.tensor
        def _(pe):
            pe.wait_ge(ident_ready, 1)
            pe.wait_ge(weights_loaded, 16 * N_WEIGHTS)

            def turn_chunk(c, s):
                pe.wait_ge(ln1_done, 2 * CT * c + CT * (s + 1))
                if s == 1 or not isinstance(c, int) or c > 0:
                    pe.wait_ge(h_copied, 2 * (2 * c + s))
                for k in range(DK):
                    for t in range(CT):
                        mm = pe.transpose(bank[k][:, t * P:(t + 1) * P], h_tok[:, s, t, k * P:(k + 1) * P],
                                          ident[:, :])
                mm.then_inc(h_turned, 1)

            def project_t(c, s, w):
                pe.wait_ge(h_copied, 2 * (2 * c + s + 1))
                if s == 1 or not isinstance(c, int) or c > 0:
                    pe.wait_ge(raw_ready, 2 * c + s)
                for m in range(DK):
                    for k in range(DK):
                        mm = pe.matmul(bank[2 + m][:, :], wqkv[:, w, k, m * P:(m + 1) * P], h_feat[:, s, k, :],
                                       start=(k == 0), stop=(k == DK - 1))
                mm.then_inc(projected, 1)

            def project_v(c):
                if not isinstance(c, int) or c > 0:
                    pe.wait_ge(v_stored, c)
                for t in range(CT):
                    for k in range(DK):
                        mm = pe.matmul(score[0][:, t * D:(t + 1) * D], h_feat[:, 0, k, t * P:(t + 1) * P],
                                       wqkv[:, 1, k, :], start=(k == 0), stop=(k == DK - 1))
                mm.then_inc(v_projected, 1)

            def prepare(c):
                turn_chunk(c, 0)
                project_t(c, 0, 0)
                turn_chunk(c, 1)
                project_v(c)
                project_t(c, 1, 2)

            prepare(0)
            with pe.Fori(1, CHUNKS) as c:
                prepare(c)

            pe.wait_ge(k_stacked, 16 * STACK_DMAS * CHUNKS)
            pe.wait_ge(v_stored, CHUNKS)
            pe.wait_ge(raw_ready, 2 * CHUNKS)
            pe.wait_ge(h_copied, 4 * CHUNKS)

            def score_half(t, h, half, first):
                if half == 0 and h % HPG == 0:
                    pe.wait_ge(q_stacked[h // HPG], 16 * STACK_DMAS * (t + 1))
                if not first:
                    pe.wait_ge(masked, 2 * (t * H + h) - 1 + half)
                for n in range(HALF // CH):
                    col = half * HALF + n * CH
                    mm = pe.matmul(score[half][:, n * CH:(n + 1) * CH], q_stack[:, h, :],
                                   k_stack[:, h, col:col + CH], start=True, stop=True)
                mm.then_inc(scores_ready, 1)

            def turn_quarter(t, h, q, first):
                u = t * H + h
                if q == 0:
                    pe.wait_ge(probs_ready, u + 1)
                if not (first and q < 2):
                    pe.wait_ge(copied_act if q % 2 == 0 else copied_dve, 2 * u + q // 2)
                for i in range(4):
                    b = 4 * q + i
                    mm = pe.transpose(turned[q % 2][:, i * P:(i + 1) * P], logits[:, h % LR, b * P:(b + 1) * P],
                                      ident[:, :])
                mm.then_inc(quarter_turned, 1)

            def weigh_half(t, h, half, first_tile):
                u = t * H + h
                if half == 0:
                    pe.wait_ge(copied_act, 2 * u + 2)
                    pe.wait_ge(copied_dve, 2 * u + 2)
                    if h % HPG == 0 and not (first_tile and h == 0):
                        pe.wait_ge(ctx_copied, GROUPS * t + h // HPG)
                for k in range(2 * half, 2 * half + 2):
                    for j in range(HPG):
                        s = HPG * k + j
                        mm = pe.matmul(ctx_ps[HD * j:HD * (j + 1), (h % HPG) * P:(h % HPG + 1) * P],
                                       v_all[:, s, h * HD:(h + 1) * HD], probs_t[:, h % 2, s, :],
                                       start=(k == 0), stop=(k == TILES // HPG - 1), skip_group_check=True)
                if half == 1:
                    mm.then_inc(ctx_done, 1)

            def turn_back(n, first):
                pe.wait_ge(ctx_copied, n + 1)
                if not first:
                    pe.wait_ge(ctx_step, 2 * n - 1)
                for i in range(HPG):
                    mm = pe.transpose(back_ps[:, i * P:(i + 1) * P], ctx_part[:, i * P:(i + 1) * P], ident[:, :])
                mm.then_inc(ctx_back, 1)

            def attend(t):
                first = isinstance(t, int) and t == 0
                last = isinstance(t, int) and t == TILES - 1
                for h in range(H):
                    hs, ts = (h + 3) % H, t + (h + 3) // H
                    hw, tw = (h - 1) % H, t + (h - 1) // H
                    more = not (last and h + 3 >= H)
                    before = not (first and h == 0)
                    turn_quarter(t, h, 0, first and h == 0)
                    if before:
                        weigh_half(tw, hw, 0, first)
                    turn_quarter(t, h, 1, first and h == 0)
                    if more:
                        score_half(ts, hs, 0, False)
                    turn_quarter(t, h, 2, first and h == 0)
                    if before:
                        weigh_half(tw, hw, 1, first)
                    turn_quarter(t, h, 3, first and h == 0)
                    if more:
                        score_half(ts, hs, 1, False)
                    if h == 5:
                        turn_back(GROUPS * t, first)
                    if h == 1 and not first:
                        turn_back(GROUPS * t - 1, False)

            for h in range(3):
                for half in range(2):
                    score_half(0, h, half, h == 0)
            attend(0)
            with pe.Fori(1, TILES - 1) as t:
                attend(t)
            attend(TILES - 1)
            weigh_half(TILES - 1, H - 1, 0, False)
            weigh_half(TILES - 1, H - 1, 1, False)
            turn_back(GROUPS * TILES - 1, False)

            pe.wait_ge(weights3_loaded, 16 * N_WEIGHTS3)

            def out_project(t, r, n, first):
                pe.wait_ge(rows_loaded[r], 48 * n)
                if first:
                    pe.wait_ge(copied_dve, 2 * UNITS)
                    pe.wait_ge(copied_act, 2 * UNITS)
                else:
                    pe.wait_ge(ctxt_copied, t)
                for k in range(DK):
                    mm = pe.transpose(turned[0][:, k * P:(k + 1) * P], in3[:, r, 0, k * P:(k + 1) * P], ident[:, :])
                mm.then_inc(ctxt_turned, 1)
                if not first:
                    pe.wait_ge(ln2_step, 8 * t - 7)
                pe.wait_ge(ctxt_copied, t + 1)
                for k in range(DK):
                    mm = pe.matmul(turned[1][:, 0:D], ctx_t[:, k, :], wo_sb[:, k, :], start=(k == 0), stop=(k == DK - 1))
                mm.then_inc(attn_ready, 1)

            def turn_h2(t, r, first):
                pe.wait_ge(ln2_step, 8 * t + 8)
                if first:
                    pe.wait_ge(ctx_copied, GROUPS * TILES)
                else:
                    pe.wait_ge(h2_copied, t)
                for k in range(DK):
                    mm = pe.transpose(ctx_ps[:, k * P:(k + 1) * P], h2[:, r, k * P:(k + 1) * P], ident[:, :])
                mm.then_inc(h2_turned, 1)

            def mlp_in(t):
                pe.wait_ge(h2_copied, t + 1)
                if isinstance(t, int) and t == 0:
                    pe.wait_ge(masked, 2 * UNITS)
                else:
                    pe.wait_ge(gelu_ready, 2 * t)
                for f in range(FK):
                    for k in range(DK):
                        mm = pe.matmul(score[0][:, f * P:(f + 1) * P], w1_sb[:, k, f * P:(f + 1) * P], h2_t[:, k, :],
                                       start=(k == 0), stop=(k == DK - 1))
                    if f % 4 == 3:
                        mm.then_inc(hidden_ready, 1)

            def mlp_out(t):
                pe.wait_ge(gelu_ready, 2 * t + 2)
                if isinstance(t, int) and t == 0:
                    pe.wait_ge(ctx_ready, GROUPS * TILES)
                else:
                    pe.wait_ge(ln3_step, 6 * t - 5)
                for f in range(FK):
                    mm = pe.matmul(back_ps[:, 0:D], gelu_t[:, f, :], w2_sb[:, f, :], start=(f == 0), stop=(f == FK - 1))
                mm.then_inc(ff_ready, 1)

            out_project(0, 0, 1, True)
            turn_h2(0, 0, True)

            def finish(i, last):
                for r in range(2):
                    t = 2 * i + r
                    mlp_in(t)
                    more = not (last and r == 1)
                    if more:
                        out_project(t + 1, 1 - r, i + 1 + r, False)
                    mlp_out(t)
                    if more:
                        turn_h2(t + 1, 1 - r, False)

            finish(0, False)
            with pe.Fori(1, TILES // 2 - 1) as i:
                finish(i, False)
            finish(TILES // 2 - 1, True)

        @block.scalar
        def _(act):
            def copy_chunk(c, s):
                act.wait_ge(h_turned, 2 * c + s + 1)
                if not isinstance(c, int) or c > 0:
                    act.wait_ge(projected, 2 * (c - 1) + s + 1)
                    if s == 0:
                        act.wait_ge(v_projected, c)
                for k in range(DK):
                    act.copy(h_feat[:, s, k, :], bank[k][:, :]).then_inc(h_copied, 1)

            def hi_part(c, s):
                act.wait_ge(raw_ready, 2 * c + s + 1)
                if s == 0:
                    if not isinstance(c, int) or c > 0:
                        act.wait_ge(k_stacked, 16 * STACK_DMAS * c)
                    act.copy(k_hi[:, :, :], raw[:, s, :, :]).then_inc(hi_ready, 1)
                else:
                    act.copy(q_hi[:, :, ds(c * CH, CH)], raw[:, s, :, :]).then_inc(hi_ready, 1)

            def prepare(c):
                copy_chunk(c, 0)
                copy_chunk(c, 1)
                hi_part(c, 0)
                hi_part(c, 1)

            prepare(0)
            with act.Fori(1, CHUNKS) as c:
                prepare(c)

            def exponential(t, h, first):
                act.wait_ge(negmax_ready, t * H + h + 1)
                if not first and h % HPG == 0:
                    act.wait_ge(ctx_ready, GROUPS * (t - 1) + h // HPG + 1)
                act.activation(logits[:, h % LR, :], logits[:, h % LR, :], ACT.Exp, bias=negmax[:, h:h + 1], scale=1.0,
                               accum_out=sums[:, h:h + 1]).then_inc(probs_ready, 1)

            def copy_quarter(t, h, q, free):
                u = t * H + h
                act.wait_ge(quarter_turned, QUARTERS * u + q + 1)
                if q == 0 and not free:
                    act.wait_ge(ctx_done, u - 1)
                act.copy(probs_t[:, h % 2, 4 * q:4 * q + 4, :].rearrange("p a b -> p (a b)"),
                         turned[q % 2][:, :]).then_inc(copied_act, 1)

            def copy_ctx(n, units, first):
                act.wait_ge(ctx_done, units)
                if not first:
                    act.wait_ge(ctx_back, n)
                act.copy(ctx_part[:, :], ctx_ps[:, :]).then_inc(ctx_copied, 1)

            def attend(t):
                first = isinstance(t, int) and t == 0
                last = isinstance(t, int) and t == TILES - 1
                for h in range(H):
                    copy_quarter(t, h, 0, first and h < 2)
                    if not (last and h + 1 == H):
                        exponential(t + (h + 1) // H, (h + 1) % H, first and h + 1 < H)
                    copy_quarter(t, h, 2, True)
                    if h == 4:
                        copy_ctx(GROUPS * t, t * H + HPG, first)
                    if h == 0 and not first:
                        copy_ctx(GROUPS * t - 1, t * H, False)

            exponential(0, 0, True)
            attend(0)
            with act.Fori(1, TILES - 1) as t:
                attend(t)
            attend(TILES - 1)
            copy_ctx(GROUPS * TILES - 1, UNITS, False)

            def copy_ctxt(t, first):
                act.wait_ge(ctxt_turned, t + 1)
                if not first:
                    act.wait_ge(attn_ready, t)
                else:
                    act.wait_ge(ctx_done, UNITS)
                act.copy(ctx_t, turned[0][:, 0:D].rearrange("p (k n) -> p k n", k=DK)).then_inc(ctxt_copied, 1)

            def copy_h2(t, first):
                act.wait_ge(h2_turned, t + 1)
                if not first:
                    act.wait_ge(hidden_ready, 2 * t)
                act.copy(h2_t, ctx_ps[:, 0:D].rearrange("p (k n) -> p k n", k=DK)).then_inc(h2_copied, 1)

            def gelu(t, half, first):
                act.wait_ge(hidden_ready, 2 * t + half + 1)
                if not first:
                    act.wait_ge(ff_ready, t)
                act.activation(gelu_t[:, 4 * half:4 * half + 4, :].rearrange("p a b -> p (a b)"),
                               score[0][:, half * CH:(half + 1) * CH], ACT.Gelu_apprx_tanh).then_inc(gelu_ready, 1)

            copy_ctxt(0, True)
            copy_h2(0, True)

            def finish(t, first, last):
                gelu(t, 0, first)
                gelu(t, 1, first)
                if not last:
                    copy_ctxt(t + 1, False)
                    copy_h2(t + 1, False)

            finish(0, True, False)
            with act.Fori(1, TILES - 1) as t:
                finish(t, False, False)
            finish(TILES - 1, False, True)

        @block.vector
        def _(dve):
            dve.wait_ge(weights_loaded, 16 * N_WEIGHTS)
            dve.tensor_scalar(node[:, :], node_i[:, :], 1.0, None, ALU.is_equal).then_inc(node_ready, 1)
            dve.wait_ge(node_ready, 1)

            def ln1_stats(c, s):
                base = 2 * CT * (2 * c + s)
                dve.wait_ge(x_loaded[s], 16 * (c + 1))
                for i in range(CT):
                    dve.bn_stats(stats[:, s, i, :], h_tok[:, s, i, :]).then_inc(stat_step, 1)
                wait_alone(dve, stat_step, base + CT)
                for i in range(CT):
                    dve.bn_aggr(moments[:, s, i, :], stats[:, s, i, :]).then_inc(stat_step, 1)
                dve.wait_ge(stat_step, base + 2 * CT)
                dve.tensor_scalar(var_eps[:, s, :], moments[:, s, :, 1], EPS, None, ALU.add).then_inc(var_ready, 1)

            def ln1_apply(c, s):
                base = 2 * CT * (2 * c + s)
                dve.wait_ge(rstd_ready, 2 * c + s + 1)
                for i in range(CT):
                    row = h_tok[:, s, i, :]
                    dve.tensor_scalar(row, row, moments[:, s, i, 0:1], rstd[:, s, i:i + 1], ALU.subtract,
                                      ALU.mult).then_inc(norm_step, 1)
                dve.wait_ge(norm_step, base + CT)
                for i in range(CT):
                    row = h_tok[:, s, i, :]
                    dve.scalar_tensor_tensor(out=row, in0=row, scalar=node[:, ds(c * CT + i, 1)], in1=ln1_bc[:, 0, :],
                                             op0=ALU.mult, op1=ALU.mult).then_inc(norm_step, 1)
                dve.wait_ge(norm_step, base + 2 * CT)
                for i in range(CT):
                    row = h_tok[:, s, i, :]
                    dve.scalar_tensor_tensor(out=row, in0=ln1_bc[:, 1, :], scalar=node[:, ds(c * CT + i, 1)], in1=row,
                                             op0=ALU.mult, op1=ALU.add).then_inc(ln1_done, 1)

            def add_bias(c, s):
                dve.wait_ge(projected, 2 * c + s + 1)
                if not isinstance(c, int) or c > 0:
                    dve.wait_ge(lo_ready, 2 * (c - 1) + s + 1)
                for m in range(DK):
                    if s == 0:
                        last = dve.tensor_scalar(raw[:, s, m, :], bank[2 + m][:, :], bqk[:, 0, m:m + 1], None, ALU.add)
                    else:
                        last = dve.tensor_scalar(raw[:, s, m, :], bank[2 + m][:, :], bqk[:, 1, m:m + 1], Q_SCALE, ALU.add,
                                                 ALU.mult)
                last.then_inc(raw_ready, 1)

            def lo_part(c, s):
                dve.wait_ge(hi_ready, 2 * c + s + 1)
                if s == 0:
                    if not isinstance(c, int) or c > 0:
                        dve.wait_ge(k_stacked, 16 * STACK_DMAS * c)
                    hi, lo = k_hi[:, :, :], k_lo[:, :, :]
                else:
                    hi, lo = q_hi[:, :, ds(c * CH, CH)], q_lo[:, :, ds(c * CH, CH)]
                dve.tensor_tensor(lo, raw[:, s, :, :], hi.bitcast(F32), ALU.subtract).then_inc(lo_ready, 1)

            def store_v(c):
                dve.wait_ge(v_projected, c + 1)
                for i in range(CT):
                    last = dve.tensor_tensor(v_all[:, ds(c * CT + i, 1), :].rearrange("p a d -> p (a d)"),
                                             score[0][:, i * D:(i + 1) * D], bv_bc, ALU.add)
                last.then_inc(v_stored, 1)

            def prepare(c):
                add_bias(c, 0)
                lo_part(c, 0)
                store_v(c)
                add_bias(c, 1)
                lo_part(c, 1)

            def ln1(c):
                ln1_stats(c, 0)
                ln1_stats(c, 1)
                ln1_apply(c, 0)
                ln1_apply(c, 1)

            ln1(0)
            prepare(0)
            with dve.Fori(1, CHUNKS) as c:
                ln1(c)
                prepare(c)

            def make_mask(t, first):
                dve.wait_ge(adj_loaded, 16 * (t + 1))
                if not first:
                    dve.wait_ge(masked, 2 * t * H)
                dve.tensor_scalar(mask_sb[:, :], adj_sb[:, :], 0.0, NEG, ALU.is_equal, ALU.mult).then_inc(mask_ready, 1)
                dve.wait_ge(mask_ready, t + 1)

            def mask_half(t, h, half, free):
                u = t * H + h
                if half == 0 and not free:
                    dve.wait_ge(quarter_turned, QUARTERS * (u - LR + 1))
                if half == 1:
                    dve.wait_ge(masked, 2 * u + 1)
                wait_alone(dve, scores_ready, 2 * u + half + 1)
                start = LOWEST if half == 0 else rowmax[:, h, 0:1]
                dve.tensor_tensor_reduce(logits[:, h % LR, half * HALF:(half + 1) * HALF], score[half][:, :],
                                         mask_sb[:, half * HALF:(half + 1) * HALF], 1.0, start, ALU.add, ALU.max,
                                         rowmax[:, h, half:half + 1]).then_inc(masked, 1)

            def negate(t, h):
                dve.wait_ge(masked, 2 * (t * H + h) + 2)
                dve.tensor_scalar(negmax[:, h:h + 1], rowmax[:, h, 1:2], -1.0, None, ALU.mult).then_inc(negmax_ready, 1)

            def copy_quarter(t, h, q, free):
                u = t * H + h
                dve.wait_ge(quarter_turned, QUARTERS * u + q + 1)
                if q == 1 and not free:
                    dve.wait_ge(ctx_done, u - 1)
                dve.tensor_copy(probs_t[:, h % 2, 4 * q:4 * q + 4, :].rearrange("p a b -> p (a b)"),
                                turned[q % 2][:, :]).then_inc(copied_dve, 1)

            def normalise(n, g, saved):
                if saved is not None:
                    dve.wait_ge(ctx_saved, saved)
                dve.wait_ge(ctx_back, n + 1)
                dve.tensor_reduce(ctx_sum[:, :, :], back_ps[:, :].rearrange("p (h j d) -> p h d j", h=HPG, j=HPG), AX.X,
                                  ALU.add).then_inc(ctx_step, 1)
                dve.reciprocal(recip[:, :], sums[:, g * HPG:(g + 1) * HPG]).then_inc(ctx_step, 1)
                dve.wait_ge(ctx_step, 2 * n + 2)
                for i in range(HPG):
                    last = dve.tensor_scalar(ctx_norm[:, (g * HPG + i) * HD:(g * HPG + i + 1) * HD], ctx_sum[:, i, :],
                                             recip[:, i:i + 1], None, ALU.mult)
                last.then_inc(ctx_ready, 1)

            def attend(t):
                first = isinstance(t, int) and t == 0
                last = isinstance(t, int) and t == TILES - 1
                for h in range(H):
                    hm, tm = (h + 2) % H, t + (h + 2) // H
                    more = not (last and h + 2 >= H)
                    free = first and h + 2 < LR
                    if more:
                        if hm == 0:
                            make_mask(tm, False)
                        mask_half(tm, hm, 0, free)
                    copy_quarter(t, h, 1, first and h < 2)
                    if more:
                        mask_half(tm, hm, 1, free)
                        negate(tm, hm)
                    copy_quarter(t, h, 3, True)
                    if h == 5:
                        normalise(GROUPS * t, 0, None if first else 16 * t)
                    if h == 1 and not first:
                        normalise(GROUPS * t - 1, 1, None)

            make_mask(0, True)
            for h in range(2):
                for half in range(2):
                    mask_half(0, h, half, True)
                negate(0, h)
            attend(0)
            with dve.Fori(1, TILES - 1) as t:
                attend(t)
            attend(TILES - 1)
            normalise(GROUPS * TILES - 1, 1, None)

            dve.wait_ge(weights3_loaded, 16 * N_WEIGHTS3)

            def row_stats(src, slot, step, base):
                dve.wait_ge(step, base)
                dve.bn_stats(stats[:, slot, 0, :], src).then_inc(step, 1)
                wait_alone(dve, step, base + 1)
                dve.bn_aggr(moments[:, slot, 0, :], stats[:, slot, 0, :]).then_inc(step, 1)
                dve.wait_ge(step, base + 2)
                dve.tensor_scalar(var_eps[:, slot, 0:1], moments[:, slot, 0, 1:2], EPS, None, ALU.add).then_inc(step, 1)

            def ln2(t, r, n, first):
                base = 8 * t
                m = node[:, ds(t, 1)]
                dve.wait_ge(attn_ready, t + 1)
                dve.wait_ge(rows_loaded[r], 48 * n)
                if first:
                    dve.wait_ge(ctx_done, UNITS)
                dve.tensor_tensor(res, turned[1][:, 0:D], bo_bc, ALU.add).then_inc(ln2_step, 1)
                dve.wait_ge(ln2_step, base + 1)
                dve.scalar_tensor_tensor(out=res, in0=res, scalar=m, in1=in3[:, r, 1, :], op0=ALU.mult,
                                         op1=ALU.add).then_inc(ln2_step, 1)
                row_stats(res, 0, ln2_step, base + 2)
                dve.wait_ge(rstd2_ready, t + 1)
                dve.tensor_scalar(res, res, moments[:, 0, 0, 0:1], rstd[:, 0, 0:1], ALU.subtract,
                                  ALU.mult).then_inc(ln2_step, 1)
                dve.wait_ge(ln2_step, base + 6)
                dve.scalar_tensor_tensor(out=res, in0=res, scalar=m, in1=scale2_bc, op0=ALU.mult,
                                         op1=ALU.mult).then_inc(ln2_step, 1)
                dve.wait_ge(ln2_step, base + 7)
                dve.scalar_tensor_tensor(out=h2[:, r, :], in0=bias2_bc, scalar=m, in1=res, op0=ALU.mult,
                                         op1=ALU.add).then_inc(ln2_step, 1)

            def ln3(t, r, n):
                base = 6 * t
                dve.wait_ge(ff_ready, t + 1)
                if not (isinstance(t, int) and t == 0):
                    dve.wait_ge(ln3_step, base)
                dve.tensor_tensor(res2, back_ps[:, 0:D], h2[:, r, :], ALU.add).then_inc(ln3_step, 1)
                dve.wait_ge(ln3_step, base + 1)
                dve.tensor_tensor(res2, res2, in3[:, r, 2, :], ALU.add).then_inc(ln3_step, 1)
                row_stats(res2, 1, ln3_step, base + 2)
                dve.wait_ge(rstd3_ready, t + 1)
                if n is not None:
                    dve.wait_ge(y_saved[r], 16 * n)
                dve.tensor_scalar(y_out[:, r, :], res2, moments[:, 1, 0, 0:1], rstd[:, 1, 0:1], ALU.subtract,
                                  ALU.mult).then_inc(ln3_step, 1)

            ln2(0, 0, 1, True)

            def finish(i, last):
                first = isinstance(i, int) and i == 0
                for r in range(2):
                    t = 2 * i + r
                    if not (last and r == 1):
                        ln2(t + 1, 1 - r, i + 1 + r, False)
                    ln3(t, r, None if first else i)

            finish(0, False)
            with dve.Fori(1, TILES // 2 - 1) as i:
                finish(i, False)
            finish(TILES // 2 - 1, True)


_INS = ["x", "adj", "nodemask", "L0_gnn_h_target", "L0_gnn_ln1_scale", "L0_gnn_ln1_bias", "L0_gnn_Wq", "L0_gnn_bq",
        "L0_gnn_Wk", "L0_gnn_bk", "L0_gnn_Wv", "L0_gnn_bv", "L0_gnn_Wo", "L0_gnn_bo", "L0_gnn_ln2_scale",
        "L0_gnn_ln2_bias", "L0_gnn_W1", "L0_gnn_W2"]


def kernel(**inputs):
    import numpy as _np
    import concourse.bacc as _bacc
    from concourse import mybir as _mybir
    from concourse.bass_utils import run_bass_kernel_spmd as _run

    nc = _bacc.Bacc("TRN2", target_bir_lowering=False, num_devices=1)
    arrays, args = {}, []
    for name in _INS:
        a = _np.ascontiguousarray(inputs[name])
        arrays[f"in_{name}_dram"] = a
        args.append(nc.dram_tensor(f"in_{name}_dram", a.shape, _mybir.dt.from_np(a.dtype), kind="ExternalInput").ap())
    shape = inputs["x"].shape
    args.append(nc.dram_tensor("out_0_dram", shape, _mybir.dt.float32, kind="ExternalOutput").ap())
    graph_attention(nc, *args)
    r = _run(nc, [arrays], core_ids=[0])
    return r.results[0]["out_0_dram"]
```

```python
from contextlib import ExitStack

import concourse.bass as bass
from concourse import mybir

ALU = mybir.AluOpType
ACT = mybir.ActivationFunctionType
AX = mybir.AxisListType
F32 = mybir.dt.float32
BF16 = mybir.dt.bfloat16
I32 = mybir.dt.int32
U32 = mybir.dt.uint32

P = 128
EPS = 1e-5
NEG = -1e30
NO_EDGE = -1e29
TINY = 1e-30
LOWEST = -3.0e38
ds = bass.ds


def graph_attention(nc, x, adj, nodemask, h_target, ln1_scale, ln1_bias, Wq, bq, Wk, bk, Wv, bv, Wo, bo,
                    ln2_scale, ln2_bias, W1, W2, out):
    N, D = x.shape
    H = 8
    HD = D // H
    DF = W1.shape[1]
    TILES = N // P
    DK = D // P
    FK = DF // P
    CH = 512
    CT = CH // P
    CHUNKS = N // CH
    Q_SCALE = 1.0 / float(HD) ** 0.5
    G = 8
    UT = 2 * G
    UNITS = N // UT
    UPT = P // UT
    SLOTS = P // 2
    SEGS = N // CH
    SEG_PICKS = 24
    CAND = SEGS * SEG_PICKS
    KV = 2 * D
    SEL = 4
    HT = H // DK * UT
    HALF = N // 2
    HPG = 4
    GROUPS = H // HPG
    QUARTERS = 4
    LR = 4
    DENSE_UNITS = TILES * H

    ctx = ExitStack()
    with ctx:
        def sb(name, shape, dt=F32):
            return ctx.enter_context(nc.sbuf_tensor(name, shape, dt))

        def sem(name):
            return ctx.enter_context(nc.semaphore(name))

        ht_dram = nc.dram_tensor("ht_scratch", (N, D), F32).ap()
        kv_dram = nc.dram_tensor("kv_scratch", (N, KV), F32).ap()
        ctx_dram = nc.dram_tensor("ctx_scratch", (N, D), F32).ap()

        ident = sb("ident", [P, P])
        ident_bf = sb("ident_bf", [P, P], BF16)
        iota = sb("iota", [P, N])
        minus_half = sb("minus_half", [P, CT])
        mean_ones = sb("mean_ones", [P, P])
        code_weights = sb("code_weights", [P, 2, UNITS + P - UPT], BF16)
        pick_rows = sb("pick_rows", [P, 2 * UT])
        head_sel = sb("head_sel", [P, H])
        quadrant = sb("quadrant", [P, HPG])
        head_block = sb("head_block", [P, D])
        node_i = sb("node_i", [P, TILES], I32)
        node = sb("node", [P, TILES])
        degree = sb("degree", [P, TILES])
        empty = sb("empty", [P, TILES])
        mean_v = sb("mean_v", [P, D])
        q_t = sb("q_t", [P, DK, N])
        mask_sb = sb("mask_sb", [P, N], BF16)
        adj_sb = sb("adj_sb", [P, 2, N], I32)
        stats = sb("stats", [P, 2, CT, 6])
        moments = sb("moments", [P, 2, CT, 2])
        var_eps = sb("var_eps", [P, 2, CT])
        rstd = sb("rstd", [P, 2, CT])
        node_rstd = sb("node_rstd", [P, 2, CT])

        h_tok = sb("h_tok", [P, 2, 2, CT, D])
        keys = h_tok[:, :, :, :, :].rearrange("p r s c d -> p r (s c d)")
        cand = sb("cand", [P, 2, SEGS, SEG_PICKS])
        picks = sb("picks", [P, 2, SLOTS])
        spill = sb("spill", [P, 2, SEGS + 1])
        spill_max = sb("spill_max", [P, 1])
        spill_all = sb("spill_all", [1, 1])
        dense_flag = sb("dense_flag", [1, 1], I32)
        picks_t = sb("picks_t", [P, UNITS], I32)
        source = sb("source", [P, UNITS], I32)
        code = sb("code", [P, UNITS], I32)
        bits = sb("bits", [P, G, UNITS], I32)
        keys_iota = q_t[:, 0, :].bitcast(I32)
        slot_mask = sb("slot_mask", [P, UNITS, UT], BF16)

        arena = sb("arena", [P, 8 * N])
        work = sb("work", [P, 4 * N])
        edges = arena[:, :].bitcast(BF16).rearrange("p (t n) -> p t n", t=TILES)
        h_feat = work[:, 0:2 * DK * CH].rearrange("p (s k n) -> p s k n", s=2, k=DK)
        at = 2 * DK * CH
        wkv = work[:, at:at + DK * KV].rearrange("p (k n) -> p k n", k=DK)
        at += DK * KV
        wq_sb = work[:, at:at + DK * D].rearrange("p (k n) -> p k n", k=DK)
        at += DK * D
        ln1_bc = work[:, at:at + 2 * D].rearrange("p (w n) -> p w n", w=2)
        at += 2 * D
        bkv_bc = work[:, at:at + KV]
        at += KV
        kv_out = work[:, at:at + CT * KV].rearrange("p (r n) -> p r n", r=CT)
        at += CT * KV
        bq_col = work[:, at:at + DK]
        bq_scaled = work[:, at + DK:at + 2 * DK]
        kv_ring = arena[:, 0:UPT * KV].rearrange("p (r n) -> p r n", r=UPT)
        at = UPT * KV
        k_t = arena[:, at:at + 2 * D].rearrange("p (r k n) -> p r k n", r=2, k=DK)
        at += 2 * D
        prob = arena[:, at:at + 2 * P].rearrange("p (r n) -> p r n", r=2)
        at += 2 * P
        prob_t = arena[:, at:at + 2 * P].rearrange("p (r n) -> p r n", r=2)
        at += 2 * P
        weighed_sb = arena[:, at:at + UPT * D].rearrange("p (r n) -> p r n", r=UPT)
        at += UPT * D
        sel_sb = arena[:, at:at + 2 * D].rearrange("p (r n) -> p r n", r=2)
        q_blocks = sb("q_blocks", [P, DK, UPT, HT])
        mask_rows = sb("mask_rows", [P, UPT, H, UT], BF16)
        source_ring = sb("source_ring", [P, UPT], U32)
        row_max = sb("row_max", [P, UPT])
        neg_max = sb("neg_max", [P, UPT])
        row_sum = sb("row_sum", [P, UPT])
        row_sum_up = sb("row_sum_up", [P, UPT])
        row_recip = sb("row_recip", [P, UPT])
        logits = arena[:, 0:LR * N].rearrange("p (r n) -> p r n", r=LR)
        probs_t = arena[:, LR * N:(LR + 2) * N].rearrange("p (r s n) -> p r s n", r=2, s=TILES)
        k_rows = arena[:, LR * N:(LR + 2) * N].rearrange("p (t n) -> p t n", t=TILES)
        v_all = arena[:, (LR + 2) * N:(LR + 4) * N].rearrange("p (t n) -> p t n", t=TILES)
        kt_all = work[:, 0:DK * N].rearrange("p (k n) -> p k n", k=DK)
        q_tile = work[:, DK * N:DK * N + DK * P].rearrange("p (k n) -> p k n", k=DK)
        rowmax = sb("rowmax", [P, H, 2])
        negmax = sb("negmax", [P, H])
        sums = sb("sums", [P, H])
        recip = sb("recip", [P, HPG])
        ctx_part = sb("ctx_part", [P, HPG * P])
        ctx_sum = sb("ctx_sum", [P, HPG, HD])
        ctx_norm = sb("ctx_norm", [P, D])
        w1_sb = sb("w1_sb", [P, DK, DF])
        w2_sb = sb("w2_sb", [P, FK, D])
        wo_sb = sb("wo_sb", [P, DK, D])
        fin_bc = sb("fin_bc", [P, 3, D])
        bo_bc, scale2_bc, bias2_bc = (fin_bc[:, w, :] for w in range(3))
        gelu_t = arena[:, 0:FK * P].rearrange("p (k n) -> p k n", k=FK)
        ctx_t = arena[:, N:N + DK * P].rearrange("p (k n) -> p k n", k=DK)
        h2_t = arena[:, N + D:N + 2 * D].rearrange("p (k n) -> p k n", k=DK)
        in3 = arena[:, 2 * N:2 * N + 6 * D].rearrange("p (r w n) -> p r w n", r=2, w=3)
        h2 = arena[:, 3 * N:3 * N + 2 * D].rearrange("p (r n) -> p r n", r=2)
        res = arena[:, 4 * N:4 * N + D]
        res2 = arena[:, 4 * N + D:4 * N + 2 * D]
        y_out = arena[:, 5 * N:5 * N + 2 * D].rearrange("p (r n) -> p r n", r=2)

        bank = [ctx.enter_context(nc.psum_tensor(f"bank{i}", [P, CH], F32)) for i in range(4)]
        score = [ctx.enter_context(nc.psum_tensor(f"score{i}", [P, HALF], F32)) for i in range(2)]
        banks = [b[:, :] for b in bank] + [score[i][:, j * CH:(j + 1) * CH] for i in range(2) for j in range(2)]
        k_ps, s_ps, p_ps, o_ps, sel_ps = banks[0:2], banks[2:4], banks[4], banks[5:7], banks[7]
        turned = bank[0:2]
        ctx_ps = bank[2]
        back_ps = bank[3]

        def dram_tiles(a):
            return a.rearrange("(c t p) d -> p c t d", p=P, t=CT)

        ln_loaded = sem("ln_loaded")
        weights_loaded = sem("weights_loaded")
        x_loaded = [[sem(f"x_loaded{s}{r}") for r in range(2)] for s in range(2)]
        adj_loaded = [sem(f"adj_loaded{r}") for r in range(2)]
        const_step = sem("const_step")
        ident_ready = sem("ident_ready")
        const_ready = sem("const_ready")
        iota_ready = sem("iota_ready")
        small_step = sem("small_step")
        node_ready = sem("node_ready")
        stat_step = sem("stat_step")
        var_ready = sem("var_ready")
        rstd_ready = sem("rstd_ready")
        stat_done = sem("stat_done")
        centred = sem("centred")
        scaled = sem("scaled")
        ln1_done = sem("ln1_done")
        ht_saved = sem("ht_saved")
        edges_ready = sem("edges_ready")
        degree_ready = sem("degree_ready")
        h_turned = sem("h_turned")
        h_copied = sem("h_copied")
        kv_projected = sem("kv_projected")
        kv_ready = sem("kv_ready")
        kv_saved = [sem(f"kv_saved{r}") for r in range(CT)]
        mean_summed = sem("mean_summed")
        q_projected = sem("q_projected")
        q_copied = sem("q_copied")
        coded = sem("coded")
        keys_ready = sem("keys_ready")
        pick_step = sem("pick_step")
        spill_turned = sem("spill_turned")
        flag_ready = sem("flag_ready")
        picks_turned = sem("picks_turned")
        mask_cleared = sem("mask_cleared")
        picks_ready = sem("picks_ready")
        source_ready = sem("source_ready")
        q_blocks_ready = sem("q_blocks_ready")
        mask_rows_ready = sem("mask_rows_ready")
        gathered = [sem(f"gathered{r}") for r in range(UPT)]
        k_turned = sem("k_turned")
        k_copied = sem("k_copied")
        scored = sem("scored")
        max_done = sem("max_done")
        neg_done = sem("neg_done")
        exp_done = sem("exp_done")
        p_turned = sem("p_turned")
        p_copied = sem("p_copied")
        weighed = sem("weighed")
        norm_step = sem("norm_step")
        o_ready = sem("o_ready")
        selected = sem("selected")
        sel_copied = sem("sel_copied")
        sel_saved = [sem(f"sel_saved{r}") for r in range(2)]
        rows_ready = sem("rows_ready")
        kt_turned = sem("kt_turned")
        kt_copied = sem("kt_copied")
        adj_again = sem("adj_again")
        mask_ready = sem("mask_ready")
        q_stacked = [sem(f"q_stacked{g}") for g in range(GROUPS)]
        scores_ready = sem("scores_ready")
        masked = sem("masked")
        negmax_ready = sem("negmax_ready")
        probs_ready = sem("probs_ready")
        quarter_turned = sem("quarter_turned")
        copied_act = sem("copied_act")
        copied_dve = sem("copied_dve")
        ctx_done = sem("ctx_done")
        ctx_copied = sem("ctx_copied")
        ctx_back = sem("ctx_back")
        ctx_step = sem("ctx_step")
        ctx_ready = sem("ctx_ready")
        ctx_saved = sem("ctx_saved")
        path_done = sem("path_done")
        weights3_loaded = sem("weights3_loaded")
        rows_loaded = [sem(f"rows_loaded{r}") for r in range(2)]
        empty_ready = sem("empty_ready")
        ctx_filled = sem("ctx_filled")
        ctxt_turned = sem("ctxt_turned")
        ctxt_copied = sem("ctxt_copied")
        attn_ready = sem("attn_ready")
        ln2_step = sem("ln2_step")
        rstd2_ready = sem("rstd2_ready")
        rstd3_ready = sem("rstd3_ready")
        h2_turned = sem("h2_turned")
        h2_copied = sem("h2_copied")
        hidden_ready = sem("hidden_ready")
        gelu_ready = sem("gelu_ready")
        ff_ready = sem("ff_ready")
        ln3_step = sem("ln3_step")
        y_saved = [sem(f"y_saved{r}") for r in range(2)]
        lone_waits = {eng.engine: sem(f"lone_waits_{n}") for n, eng in (("sp", nc.sync), ("dve", nc.vector), ("pool", nc.gpsimd))}

        block = ctx.enter_context(nc.Block())
        N_LN = 3
        N_WEIGHTS = 7
        N_WEIGHTS3 = 6
        ENGINES = 5
        ROUNDS = SEG_PICKS // 8
        SPILL_STEP = 2 * (SEGS * (2 * ROUNDS - 1) + 2 * (SLOTS // 8) - 1 + 2) + 1
        KEYS = 2 * SEGS

        def wait_alone(eng, semaphore, value):
            eng.wait_ge(semaphore, value)
            eng.sem_inc(lone_waits[eng.engine], 1)

        def is_first(t):
            return isinstance(t, int) and t == 0

        def is_last(t):
            return isinstance(t, int) and t == TILES - 1

        def read_flag(eng):
            eng.wait_ge(flag_ready, 1)
            return eng.value_load(dense_flag[0:1, 0:1], min_val=0, max_val=1)

        def tiles_loop(eng, body):
            body(0)
            with eng.Fori(1, TILES - 1) as t:
                body(t)
            body(TILES - 1)

        @block.sync
        def _(sp):
            sp.dma_start(node_i[:, :], nodemask.rearrange("(t p) -> p t", p=P),
                         allow_slow_non_contiguous=True).then_inc(ln_loaded, 16)
            for w, a in enumerate((ln1_scale, ln1_bias)):
                sp.dma_start(ln1_bc[:, w, :], a.partition_broadcast(P)).then_inc(ln_loaded, 16)

            def load_x(s, c):
                src = dram_tiles(x if s == 0 else h_target)
                sp.dma_start(h_tok[:, c % 2, s, :, :], src[:, c, :, :]).then_inc(x_loaded[s][c % 2], 16)

            def load_adj(t):
                sp.dma_start(adj_sb[:, t % 2, :], adj[t * P:(t + 1) * P, :]).then_inc(adj_loaded[t % 2], 16)

            def load_w(dst, a):
                sp.dma_start(dst, a.rearrange("(k p) n -> p k n", p=P)).then_inc(weights_loaded, 16)

            for s in range(2):
                load_x(s, 0)
            load_w(wkv[:, :, 0:D], Wk)
            load_w(wkv[:, :, D:KV], Wv)
            load_adj(0)
            load_w(wq_sb, Wq)
            sp.dma_start(bkv_bc[:, 0:D], bk.partition_broadcast(P)).then_inc(weights_loaded, 16)
            sp.dma_start(bkv_bc[:, D:KV], bv.partition_broadcast(P)).then_inc(weights_loaded, 16)
            sp.dma_start(bq_col, bq.rearrange("(k p) -> p k", p=P),
                         allow_slow_non_contiguous=True).then_inc(weights_loaded, 16)
            sp.dma_start(fin_bc[:, 0, :], bo.partition_broadcast(P)).then_inc(weights_loaded, 16)
            load_adj(1)
            for s in range(2):
                load_x(s, 1)

            def save_kv(c):
                for i in range(CT):
                    t = CT * c + i
                    sp.wait_ge(kv_ready, t + 1)
                    sp.dma_start(kv_dram[t * P:(t + 1) * P, :], kv_out[:, i, :]).then_inc(kv_saved[i], 16)

            def next_adj(t):
                if t < TILES:
                    sp.wait_ge(edges_ready, t - 1)
                    load_adj(t)

            for c in range(CHUNKS):
                next_adj(CT * c + 2)
                if c > 0:
                    save_kv(c - 1)
                next_adj(CT * c + 3)
                sp.wait_ge(ln1_done, 2 * CT * (c + 1))
                sp.dma_start(dram_tiles(ht_dram)[:, c, :, :], h_tok[:, c % 2, 1, :, :]).then_inc(ht_saved, 16)
                if c + 2 < CHUNKS:
                    for s in range(2):
                        sp.wait_ge(h_turned, 2 * c + s + 1)
                        if s == 1:
                            sp.wait_ge(ht_saved, 16 * (c + 1))
                        load_x(s, c + 2)
                next_adj(CT * c + 4)
                next_adj(CT * c + 5)
            save_kv(CHUNKS - 1)
            for dst, a in ((w1_sb, W1), (w2_sb, W2), (wo_sb, Wo)):
                sp.dma_start(dst[:, :, :], a.rearrange("(k p) n -> p k n", p=P)).then_inc(weights3_loaded, 16)
            for w, a in enumerate((bo, ln2_scale, ln2_bias)):
                if w == 0:
                    sp.wait_ge(weights_loaded, 16 * N_WEIGHTS)
                sp.dma_start(fin_bc[:, w, :], a.partition_broadcast(P)).then_inc(weights3_loaded, 16)

            flag = read_flag(sp)
            with sp.If(flag == 0):
                def save_selected(k, slot):
                    wait_alone(sp, sel_copied, k + 1)
                    for j in range(SEL):
                        sp.dma_start(ctx_dram[ds(k * SEL * UT + j * UT, UT), :],
                                     sel_sb[32 * j:32 * j + UT, slot, :]).then_inc(sel_saved[slot], 16)

                for slot in range(2):
                    sp.sem_inc(sel_saved[slot], 1)
                with sp.Fori(0, TILES) as t:
                    for slot in range(2):
                        save_selected(2 * t + slot, slot)
                for slot in range(2):
                    sp.wait_ge(sel_saved[slot], 16 * SEL * TILES + 1)
                sp.sem_inc(path_done, 1)
            with sp.Else():
                for r in range(CT):
                    sp.wait_ge(kv_saved[r], 16 * CHUNKS)
                sp.wait_ge(coded, KEYS)
                sp.wait_ge(degree_ready, TILES)
                kv_rows = kv_dram.rearrange("(t p) n -> p t n", p=P)
                sp.dma_start(k_rows, kv_rows[:, :, 0:D]).then_inc(rows_ready, 16)
                sp.dma_start(v_all, kv_rows[:, :, D:KV]).then_inc(rows_ready, 16)
                sp.dma_start(adj_sb[:, 0, :], adj[0:P, :]).then_inc(adj_again, 16)
                sp.wait_ge(kv_projected, TILES)
                sp.wait_ge(q_copied, DK * CHUNKS)

                def load_q(t, g):
                    sp.dma_start(q_tile[:, g, :], q_t[:, g, ds(t * P, P)]).then_inc(q_stacked[g], 16)

                for g in range(GROUPS):
                    load_q(0, g)

                def attend(t):
                    if not is_last(t):
                        wait_alone(sp, mask_ready, t + 1)
                        sp.dma_start(adj_sb[:, 0, :], adj[ds((t + 1) * P, P), :]).then_inc(adj_again, 16)
                        for g in range(GROUPS):
                            wait_alone(sp, scores_ready, 2 * (t * H + HPG * (g + 1)))
                            load_q(t + 1, g)
                    wait_alone(sp, ctx_ready, GROUPS * (t + 1))
                    sp.dma_start(ctx_dram[ds(t * P, P), :], ctx_norm[:, :]).then_inc(ctx_saved, 16)

                with sp.Fori(0, TILES - 1) as t:
                    attend(t)
                attend(TILES - 1)
                sp.wait_ge(ctx_saved, 16 * TILES)
                sp.sem_inc(path_done, 1)

            sp.wait_ge(path_done, ENGINES)
            sp.wait_ge(ht_saved, 16 * CHUNKS)

            def load_rows(t, r):
                for w, a in enumerate((ctx_dram, ht_dram, x)):
                    sp.dma_start(in3[:, r, w, :], a[ds(t * P, P), :]).then_inc(rows_loaded[r], 16)

            def save_rows(t, r):
                wait_alone(sp, ln3_step, 6 * t + 6)
                sp.dma_start(out[ds(t * P, P), :], y_out[:, r, :]).then_inc(y_saved[r], 16)

            load_rows(0, 0)
            load_rows(1, 1)

            def finish(i, last):
                for r in range(2):
                    save_rows(2 * i + r, r)
                    if not last:
                        load_rows(2 * i + 2 + r, r)

            with sp.Fori(0, TILES // 2 - 1) as i:
                finish(i, False)
            finish(TILES // 2 - 1, True)
            for r in range(2):
                sp.wait_ge(y_saved[r], 16 * (TILES // 2))
            for r in range(CT):
                sp.wait_ge(kv_saved[r], 16 * CHUNKS)

        @block.gpsimd
        def _(pool):
            def select_step(n, out_ap, pattern, base, fill):
                pool.wait_ge(const_step, n)
                pool.affine_select(out=out_ap, in_=out_ap, compare_op=ALU.not_equal, fill=fill, base=base,
                                   pattern=pattern, channel_multiplier=1).then_inc(const_step, 1)

            pool.memset(ident[:, :], 0.0).then_inc(const_step, 1)
            select_step(1, ident[:, :], [[-1, P]], 0, 1.0)
            pool.wait_ge(const_step, 2)
            pool.memset(minus_half[:, :], -0.5).then_inc(ident_ready, 1)
            pool.wait_ge(ident_ready, 1)

            def rsqrt1(n):
                s = n % 2
                pool.wait_ge(var_ready, n + 1)
                pool.tensor_tensor(rstd[:, s, :], var_eps[:, s, :], minus_half[:, :], ALU.pow).then_inc(rstd_ready, 1)

            def scale1(c, s):
                pool.wait_ge(centred, CT * (2 * c + s + 1))
                rows = h_tok[:, c % 2, s, :, :]
                pool.tensor_tensor(rows, rows, ln1_bc[:, 0:1, :].to_broadcast([P, CT, D]), ALU.mult).then_inc(scaled, 1)

            def constants():
                pool.iota(keys_iota, pattern=[[1, N]], base=0,
                          channel_multiplier=0).then_inc(iota_ready, 1)
                pool.memset(mean_ones[:, :], 1.0 / N).then_inc(const_ready, 1)
                pool.memset(code_weights[:, :, :], 0.0).then_inc(const_step, 1)
                n = 3
                for g in range(2):
                    for b in range(G):
                        select_step(n, code_weights[:, g, P - UPT:P], [[-UT, UPT]], -(G * g + b), float(2 ** b))
                        n += 1
                pool.wait_ge(const_step, n)
                pool.memset(slot_mask[:, :, :], NEG).then_inc(mask_cleared, 1)
                pool.memset(pick_rows[:, :], 0.0).then_inc(const_ready, 1)

            for c in range(CHUNKS):
                for s in range(2):
                    rsqrt1(2 * c + s)
                for s in range(2):
                    scale1(c, s)
                if c == 0:
                    constants()

            flag = read_flag(pool)
            with pool.If(flag == 0):
                pool.wait_ge(picks_ready, 1)
                pool.wait_ge(q_copied, DK * CHUNKS)
                pool.wait_ge(coded, KEYS)
                for r in range(CT):
                    pool.wait_ge(kv_saved[r], 16 * CHUNKS)

                def fill_q(half, slot, first):
                    if not first:
                        pool.wait_ge(scored, SEL * (half - 1))
                    for k in range(DK):
                        q_units = q_t[:, k, ds(half * SEL * UT, SEL * UT)].rearrange("p (u a t) -> p u a t", u=SEL, a=1)
                        pool.tensor_tensor(
                            q_blocks[:, k, slot:slot + SEL, :].rearrange("p u (q t) -> p u q t", q=HPG),
                            q_units.to_broadcast([P, SEL, HPG, UT]),
                            quadrant[:, :].rearrange("p (a q b) -> p a q b", a=1, b=1).to_broadcast([P, SEL, HPG, UT]),
                            ALU.mult).then_inc(q_blocks_ready, 1)

                def gather(t, h):
                    u = t * UPT + h
                    if h % SEL == 0:
                        if not is_first(t):
                            pool.wait_ge(gathered[h + SEL - 1], 16 * t)
                        pool.tensor_copy(source_ring[:, h:h + SEL], source[:, ds(u, SEL)].bitcast(U32)).then_inc(
                            source_ready, 1)
                        wait_alone(pool, source_ready, 2 * t + h // SEL + 1)
                    if not is_first(t):
                        wait_alone(pool, weighed, u - UPT + 1)
                    pool.indirect_dma_start(kv_ring[:, h, :], None, kv_dram[:, :],
                                            bass.IndirectOffsetOnAxis(ap=source_ring[:, h:h + 1], axis=0)).then_inc(
                                                gathered[h], 16)

                def sparse(t):
                    for h in range(UPT):
                        gather(t, h)
                        if h == 2:
                            fill_q(2 * t + 1, SEL, is_first(t))
                        if h == 6 and not is_last(t):
                            fill_q(2 * t + 2, 0, False)

                fill_q(0, 0, True)
                tiles_loop(pool, sparse)
                pool.wait_ge(q_blocks_ready, DK * 2 * TILES)
                pool.sem_inc(path_done, 1)
            with pool.Else():
                pool.sem_inc(path_done, 1)

            pool.wait_ge(path_done, ENGINES)

            def rsqrt2(t):
                pool.wait_ge(ln2_step, 8 * t + 5)
                pool.tensor_tensor(rstd[:, 0, 0:1], var_eps[:, 0, 0:1], minus_half[:, 0:1], ALU.pow).then_inc(rstd2_ready, 1)

            def rsqrt3(t):
                pool.wait_ge(ln3_step, 6 * t + 5)
                pool.tensor_tensor(rstd[:, 1, 0:1], var_eps[:, 1, 0:1], minus_half[:, 0:1], ALU.pow).then_inc(rstd3_ready, 1)

            rsqrt2(0)
            with pool.Fori(0, TILES - 1) as t:
                rsqrt2(t + 1)
                rsqrt3(t)
            rsqrt3(TILES - 1)

        @block.tensor
        def _(pe):
            pe.wait_ge(ident_ready, 1)

            def turn_chunk(c, s):
                pe.wait_ge(ln1_done, CT * (2 * c + s + 1))
                if c > 0:
                    pe.wait_ge(h_copied, DK * (2 * c + s - 1))
                for k in range(DK):
                    for t in range(CT):
                        mm = pe.transpose(banks[2 * s + k][:, t * P:(t + 1) * P],
                                          h_tok[:, c % 2, s, t, k * P:(k + 1) * P], ident[:, :])
                mm.then_inc(h_turned, 1)

            def sum_mean(c):
                for i in range(CT):
                    t = CT * c + i
                    pe.wait_ge(kv_ready, t + 1)
                    pe.matmul(banks[7][:, 0:D], mean_ones[:, :], kv_out[:, i, D:KV], start=(t == 0),
                              stop=(t == TILES - 1)).then_inc(mean_summed, 1)

            def project_kv(c):
                pe.wait_ge(h_copied, DK * (2 * c + 1))
                for i in range(CT):
                    t = CT * c + i
                    if t >= 2:
                        pe.wait_ge(kv_ready, t - 1)
                    for k in range(DK):
                        mm = pe.matmul(banks[4 + t % 2], h_feat[:, 0, k, i * P:(i + 1) * P], wkv[:, k, :],
                                       start=(k == 0), stop=(k == DK - 1))
                    mm.then_inc(kv_projected, 1)

            def project_q(c):
                pe.wait_ge(h_copied, DK * (2 * c + 2))
                for m in range(DK):
                    if c > 0 or m > 0:
                        pe.wait_ge(q_copied, DK * c + m)
                    for k in range(DK):
                        mm = pe.matmul(banks[6], wq_sb[:, k, m * P:(m + 1) * P], h_feat[:, 1, k, :],
                                       start=(k == 0), stop=(k == DK - 1))
                    mm.then_inc(q_projected, 1)

            pe.wait_ge(const_ready, 1)
            for c in range(CHUNKS):
                turn_chunk(c, 0)
                turn_chunk(c, 1)
                if c == 0:
                    pe.wait_ge(weights_loaded, 16 * N_WEIGHTS)
                else:
                    sum_mean(c - 1)
                project_kv(c)
                project_q(c)

            pe.wait_ge(mask_cleared, 1)
            for g in range(2):
                for n in range(SEGS):
                    i = SEGS * g + n
                    if i < 2:
                        pe.wait_ge(h_copied, 2 * DK * CHUNKS)
                    else:
                        pe.wait_ge(keys_ready, i - 1)
                    for t in range(TILES):
                        if i == 0:
                            pe.wait_ge(edges_ready, t + 1)
                        mm = pe.matmul(banks[i % 2], code_weights[:, g, P - UPT * (t + 1):2 * P - UPT * (t + 1)],
                                       edges[:, t, n * CH:(n + 1) * CH], start=(t == 0), stop=(t == TILES - 1))
                    mm.then_inc(coded, 1)
                if g == 0:
                    sum_mean(CHUNKS - 1)
            pe.wait_ge(pick_step, SPILL_STEP)
            pe.transpose(banks[2][0:1, 0:P], spill_max[:, :], ident[:, :]).then_inc(spill_turned, 1)
            pe.transpose(banks[3][:, 0:P], picks[:, :, :].rearrange("p g s -> p (g s)"), ident[:, :]).then_inc(
                picks_turned, 1)

            flag = read_flag(pe)
            with pe.If(flag == 0):
                def turn_k(t, v):
                    u, h = t * UPT + v, v % UPT
                    pe.wait_ge(gathered[h], 16 * (t + v // UPT + 1))
                    if not (is_first(t) and v < 2):
                        pe.wait_ge(k_copied, u - 1)
                    for k in range(DK):
                        mm = pe.transpose(k_ps[v % 2][:, k * P:(k + 1) * P], kv_ring[:, h, k * P:(k + 1) * P], ident[:, :])
                    mm.then_inc(k_turned, 1)

                def scores(t, v):
                    u, h = t * UPT + v, v % UPT
                    if v % SEL == 0:
                        pe.wait_ge(q_blocks_ready, DK * (2 * t + v // SEL + 1))
                        pe.wait_ge(mask_rows_ready, 2 * t + v // SEL + 1)
                    pe.wait_ge(k_copied, u + 1)
                    if not (is_first(t) and v < 2):
                        pe.wait_ge(exp_done, u - 1)
                    pe.matmul(s_ps[v % 2][:, 0:P], mask_rows[:, h, :, :].rearrange("p a b -> p (a b)"), ident_bf[:, :],
                              start=True, stop=False, skip_group_check=True)
                    for k in range(DK):
                        mm = pe.matmul(s_ps[v % 2][HT * k:HT * (k + 1), 0:P], q_blocks[:, k, h, :], k_t[:, v % 2, k, :],
                                       start=False, stop=True, skip_group_check=True)
                    mm.then_inc(scored, 1)

                def turn_p(t, v):
                    u = t * UPT + v
                    pe.wait_ge(exp_done, u + 1)
                    if not (is_first(t) and v == 0):
                        pe.wait_ge(p_copied, u)
                    pe.transpose(p_ps[:, 0:P], prob[:, v % 2, :], ident[:, :]).then_inc(p_turned, 1)

                def weigh(t, v):
                    u, h = t * UPT + v, v % UPT
                    pe.wait_ge(p_copied, u + 1)
                    if not (is_first(t) and v < 2):
                        pe.wait_ge(o_ready, u - 1)
                    pe.matmul(o_ps[v % 2][:, 0:D], prob_t[:, v % 2, :], kv_ring[:, h, D:KV], start=True,
                              stop=True).then_inc(weighed, 1)

                def select(t, v, first):
                    k = (t * UPT + v) // SEL if isinstance(t, int) else 2 * t + v // SEL
                    pe.wait_ge(o_ready, SEL * (k + 1))
                    if not first:
                        pe.wait_ge(sel_copied, k)
                    for j in range(SEL):
                        mm = pe.matmul(sel_ps[32 * j:32 * (j + 1), 0:D], pick_rows[:, :], weighed_sb[:, (v + j) % UPT, :],
                                       start=True, stop=True, skip_group_check=True)
                    mm.then_inc(selected, 1)

                def sparse(t):
                    for h in range(UPT):
                        turn_p(t, h)
                        if h > 0:
                            weigh(t, h - 1)
                        elif not is_first(t):
                            weigh(t - 1, UPT - 1)
                        if not (is_last(t) and h + 2 >= UPT):
                            scores(t + (h + 2) // UPT, (h + 2) % UPT)
                        if not (is_last(t) and h + 3 >= UPT):
                            turn_k(t + (h + 3) // UPT, (h + 3) % UPT)
                        if h == 1 and not is_first(t):
                            select(t - 1, SEL, False)
                        if h == 5:
                            select(t, 0, is_first(t))

                pe.wait_ge(small_step, 5)
                turn_k(0, 0)
                turn_k(0, 1)
                scores(0, 0)
                turn_k(0, 2)
                scores(0, 1)
                tiles_loop(pe, sparse)
                weigh(TILES - 1, UPT - 1)
                select(TILES - 1, SEL, False)
                pe.wait_ge(sel_copied, 2 * TILES)
                pe.sem_inc(path_done, 1)
            with pe.Else():
                pe.wait_ge(rows_ready, 32)
                for t in range(TILES):
                    for k in range(DK):
                        if t * DK + k >= 2:
                            pe.wait_ge(kt_copied, t * DK + k - 1)
                        pe.transpose(banks[k][:, 0:P], k_rows[:, t, k * P:(k + 1) * P], ident[:, :]).then_inc(kt_turned, 1)
                pe.wait_ge(kt_copied, DK * TILES)

                def score_half(t, h, half, first):
                    rows = slice(HD * (h % HPG), HD * (h % HPG + 1))
                    if half == 0 and h % HPG == 0:
                        pe.wait_ge(q_stacked[h // HPG], 16 * (t + 1))
                    if not first:
                        pe.wait_ge(masked, 2 * (t * H + h) - 1 + half)
                    for n in range(HALF // CH):
                        col = half * HALF + n * CH
                        mm = pe.matmul(score[half][:, n * CH:(n + 1) * CH], q_tile[rows, h // HPG, :],
                                       kt_all[rows, h // HPG, col:col + CH], start=True, stop=True)
                    mm.then_inc(scores_ready, 1)

                def turn_quarter(t, h, q, first):
                    u = t * H + h
                    if q == 0:
                        pe.wait_ge(probs_ready, u + 1)
                    if not (first and q < 2):
                        pe.wait_ge(copied_act if q % 2 == 0 else copied_dve, 2 * u + q // 2)
                    for i in range(4):
                        b = 4 * q + i
                        mm = pe.transpose(turned[q % 2][:, i * P:(i + 1) * P], logits[:, h % LR, b * P:(b + 1) * P],
                                          ident[:, :])
                    mm.then_inc(quarter_turned, 1)

                def weigh_half(t, h, half, first_tile):
                    u = t * H + h
                    if half == 0:
                        pe.wait_ge(copied_act, 2 * u + 2)
                        pe.wait_ge(copied_dve, 2 * u + 2)
                        if h % HPG == 0 and not (first_tile and h == 0):
                            pe.wait_ge(ctx_copied, GROUPS * t + h // HPG)
                    for k in range(2 * half, 2 * half + 2):
                        for j in range(HPG):
                            s = HPG * k + j
                            mm = pe.matmul(ctx_ps[HD * j:HD * (j + 1), (h % HPG) * P:(h % HPG + 1) * P],
                                           v_all[:, s, h * HD:(h + 1) * HD], probs_t[:, h % 2, s, :],
                                           start=(k == 0), stop=(k == TILES // HPG - 1), skip_group_check=True)
                    if half == 1:
                        mm.then_inc(ctx_done, 1)

                def turn_back(n, first):
                    pe.wait_ge(ctx_copied, n + 1)
                    if not first:
                        pe.wait_ge(ctx_step, 2 * n - 1)
                    for i in range(HPG):
                        mm = pe.transpose(back_ps[:, i * P:(i + 1) * P], ctx_part[:, i * P:(i + 1) * P], ident[:, :])
                    mm.then_inc(ctx_back, 1)

                def attend(t):
                    first = isinstance(t, int) and t == 0
                    last = isinstance(t, int) and t == TILES - 1
                    for h in range(H):
                        hs, ts = (h + 3) % H, t + (h + 3) // H
                        hw, tw = (h - 1) % H, t + (h - 1) // H
                        more = not (last and h + 3 >= H)
                        before = not (first and h == 0)
                        turn_quarter(t, h, 0, first and h == 0)
                        if before:
                            weigh_half(tw, hw, 0, first)
                        turn_quarter(t, h, 1, first and h == 0)
                        if more:
                            score_half(ts, hs, 0, False)
                        turn_quarter(t, h, 2, first and h == 0)
                        if before:
                            weigh_half(tw, hw, 1, first)
                        turn_quarter(t, h, 3, first and h == 0)
                        if more:
                            score_half(ts, hs, 1, False)
                        if h == 5:
                            turn_back(GROUPS * t, first)
                        if h == 1 and not first:
                            turn_back(GROUPS * t - 1, False)

                for h in range(3):
                    for half in range(2):
                        score_half(0, h, half, h == 0)
                attend(0)
                with pe.Fori(1, TILES - 1) as t:
                    attend(t)
                attend(TILES - 1)
                weigh_half(TILES - 1, H - 1, 0, False)
                weigh_half(TILES - 1, H - 1, 1, False)
                turn_back(GROUPS * TILES - 1, False)
                pe.wait_ge(ctx_back, GROUPS * TILES)
                pe.sem_inc(path_done, 1)

            pe.wait_ge(path_done, ENGINES)
            pe.wait_ge(weights3_loaded, 16 * N_WEIGHTS3)

            def out_project(t, r, first):
                pe.wait_ge(ctx_filled, t + 1)
                if not first:
                    pe.wait_ge(ctxt_copied, t)
                for k in range(DK):
                    mm = pe.transpose(turned[0][:, k * P:(k + 1) * P], in3[:, r, 0, k * P:(k + 1) * P], ident[:, :])
                mm.then_inc(ctxt_turned, 1)
                if not first:
                    pe.wait_ge(ln2_step, 8 * t - 7)
                pe.wait_ge(ctxt_copied, t + 1)
                for k in range(DK):
                    mm = pe.matmul(turned[1][:, 0:D], ctx_t[:, k, :], wo_sb[:, k, :], start=(k == 0),
                                   stop=(k == DK - 1))
                mm.then_inc(attn_ready, 1)

            def turn_h2(t, r, first):
                pe.wait_ge(ln2_step, 8 * t + 8)
                if not first:
                    pe.wait_ge(h2_copied, t)
                for k in range(DK):
                    mm = pe.transpose(ctx_ps[:, k * P:(k + 1) * P], h2[:, r, k * P:(k + 1) * P], ident[:, :])
                mm.then_inc(h2_turned, 1)

            def mlp_in(t):
                pe.wait_ge(h2_copied, t + 1)
                if not is_first(t):
                    pe.wait_ge(gelu_ready, 2 * t)
                for f in range(FK):
                    for k in range(DK):
                        mm = pe.matmul(score[0][:, f * P:(f + 1) * P], w1_sb[:, k, f * P:(f + 1) * P], h2_t[:, k, :],
                                       start=(k == 0), stop=(k == DK - 1))
                    if f % 4 == 3:
                        mm.then_inc(hidden_ready, 1)

            def mlp_out(t):
                pe.wait_ge(gelu_ready, 2 * t + 2)
                if not is_first(t):
                    pe.wait_ge(ln3_step, 6 * t - 5)
                for f in range(FK):
                    mm = pe.matmul(back_ps[:, 0:D], gelu_t[:, f, :], w2_sb[:, f, :], start=(f == 0), stop=(f == FK - 1))
                mm.then_inc(ff_ready, 1)

            out_project(0, 0, True)
            turn_h2(0, 0, True)

            def finish(i, last):
                for r in range(2):
                    t = 2 * i + r
                    mlp_in(t)
                    more = not (last and r == 1)
                    if more:
                        out_project(t + 1, 1 - r, False)
                    mlp_out(t)
                    if more:
                        turn_h2(t + 1, 1 - r, False)

            finish(0, False)
            with pe.Fori(1, TILES // 2 - 1) as i:
                finish(i, False)
            finish(TILES // 2 - 1, True)


        @block.scalar
        def _(act):
            def copy_chunk(c, s):
                act.wait_ge(h_turned, 2 * c + s + 1)
                if c > 0:
                    act.wait_ge(kv_projected if s == 0 else q_projected, (CT if s == 0 else DK) * c)
                for k in range(DK):
                    act.copy(h_feat[:, s, k, :], banks[2 * s + k]).then_inc(h_copied, 1)

            def count_edges(t):
                act.wait_ge(edges_ready, t + 1)
                if t > 0:
                    act.wait_ge(degree_ready, t)
                act.activation(mask_sb[:, :], edges[:, t, :], ACT.Identity, bias=0.0, scale=1.0,
                               accum_out=degree[:, t:t + 1]).then_inc(degree_ready, 1)

            def copy_q(c):
                for m in range(DK):
                    act.wait_ge(q_projected, DK * c + m + 1)
                    act.activation(q_t[:, m, c * CH:(c + 1) * CH], banks[6], ACT.Identity, bias=bq_scaled[:, m:m + 1],
                                   scale=Q_SCALE).then_inc(q_copied, 1)

            act.wait_ge(node_ready, 3)
            for c in range(CHUNKS):
                copy_chunk(c, 0)
                copy_chunk(c, 1)
                if c > 0:
                    for i in range(CT):
                        count_edges(CT * (c - 1) + i)
                copy_q(c)
            for i in range(CT):
                count_edges(CT * (CHUNKS - 1) + i)

            flag = read_flag(act)
            with act.If(flag == 0):
                def spread_mask(half, slot, first):
                    if not first:
                        act.wait_ge(scored, SEL * (half - 1))
                    src = slot_mask[:, ds(half * SEL, SEL), :].rearrange("p u (a t) -> p u a t", a=1)
                    act.copy(mask_rows[:, slot:slot + SEL, :, :],
                             src.to_broadcast([P, SEL, H, UT])).then_inc(mask_rows_ready, 1)

                def copy_k(t, v):
                    u = t * UPT + v
                    act.wait_ge(k_turned, u + 1)
                    if not (is_first(t) and v < 2):
                        act.wait_ge(scored, u - 1)
                    act.copy(k_t[:, v % 2, :, :].rearrange("p k n -> p (k n)"), k_ps[v % 2][:, 0:D]).then_inc(k_copied, 1)

                def exponential(t, v):
                    u, h = t * UPT + v, v % UPT
                    act.wait_ge(neg_done, u + 1)
                    if not (is_first(t) and v < 2):
                        act.wait_ge(p_turned, u - 1)
                    act.activation(prob[:, v % 2, :], s_ps[v % 2][:, 0:P], ACT.Exp, bias=neg_max[:, h:h + 1], scale=1.0,
                                   accum_out=row_sum[:, h:h + 1]).then_inc(exp_done, 1)

                def copy_selected(t, slot):
                    k = 2 * t + slot
                    act.wait_ge(selected, k + 1)
                    if not is_first(t):
                        act.wait_ge(sel_saved[slot], 16 * SEL * t + 1)
                    act.copy(sel_sb[:, slot, :], sel_ps[:, 0:D]).then_inc(sel_copied, 1)

                def sparse(t):
                    for h in range(UPT):
                        if not (is_last(t) and h + 1 >= UPT):
                            exponential(t + (h + 1) // UPT, (h + 1) % UPT)
                        if not (is_last(t) and h + 3 >= UPT):
                            copy_k(t + (h + 3) // UPT, (h + 3) % UPT)
                        if h == 0:
                            spread_mask(2 * t + 1, SEL, is_first(t))
                        if h == 4 and not is_last(t):
                            spread_mask(2 * t + 2, 0, False)
                        if h == 2 and not is_first(t):
                            copy_selected(t - 1, 1)
                        if h == 6:
                            copy_selected(t, 0)

                act.wait_ge(picks_ready, 1)
                spread_mask(0, 0, True)
                copy_k(0, 0)
                copy_k(0, 1)
                exponential(0, 0)
                copy_k(0, 2)
                tiles_loop(act, sparse)
                copy_selected(TILES - 1, 1)
                act.sem_inc(path_done, 1)
            with act.Else():
                act.wait_ge(picks_ready, 1)
                for t in range(TILES):
                    for k in range(DK):
                        act.wait_ge(kt_turned, t * DK + k + 1)
                        act.copy(kt_all[:, k, t * P:(t + 1) * P], banks[k][:, 0:P]).then_inc(kt_copied, 1)

                def exponential(t, h, first):
                    act.wait_ge(negmax_ready, t * H + h + 1)
                    if not first and h % HPG == 0:
                        act.wait_ge(ctx_ready, GROUPS * (t - 1) + h // HPG + 1)
                    act.activation(logits[:, h % LR, :], logits[:, h % LR, :], ACT.Exp, bias=negmax[:, h:h + 1], scale=1.0,
                                   accum_out=sums[:, h:h + 1]).then_inc(probs_ready, 1)

                def copy_quarter(t, h, q, free):
                    u = t * H + h
                    act.wait_ge(quarter_turned, QUARTERS * u + q + 1)
                    if q == 0 and not free:
                        act.wait_ge(ctx_done, u - 1)
                    act.copy(probs_t[:, h % 2, 4 * q:4 * q + 4, :].rearrange("p a b -> p (a b)"),
                             turned[q % 2][:, :]).then_inc(copied_act, 1)

                def copy_ctx(n, units, first):
                    act.wait_ge(ctx_done, units)
                    if not first:
                        act.wait_ge(ctx_back, n)
                    act.copy(ctx_part[:, :], ctx_ps[:, :]).then_inc(ctx_copied, 1)

                def attend(t):
                    first = isinstance(t, int) and t == 0
                    last = isinstance(t, int) and t == TILES - 1
                    for h in range(H):
                        copy_quarter(t, h, 0, first and h < 2)
                        if not (last and h + 1 == H):
                            exponential(t + (h + 1) // H, (h + 1) % H, first and h + 1 < H)
                        copy_quarter(t, h, 2, True)
                        if h == 4:
                            copy_ctx(GROUPS * t, t * H + HPG, first)
                        if h == 0 and not first:
                            copy_ctx(GROUPS * t - 1, t * H, False)

                exponential(0, 0, True)
                attend(0)
                with act.Fori(1, TILES - 1) as t:
                    attend(t)
                attend(TILES - 1)
                copy_ctx(GROUPS * TILES - 1, DENSE_UNITS, False)
                act.wait_ge(ctx_copied, GROUPS * TILES)
                act.sem_inc(path_done, 1)

            act.wait_ge(path_done, ENGINES)

            def copy_ctxt(t, first):
                act.wait_ge(ctxt_turned, t + 1)
                if not first:
                    act.wait_ge(attn_ready, t)
                act.copy(ctx_t, turned[0][:, 0:D].rearrange("p (k n) -> p k n", k=DK)).then_inc(ctxt_copied, 1)

            def copy_h2(t, first):
                act.wait_ge(h2_turned, t + 1)
                if not first:
                    act.wait_ge(hidden_ready, 2 * t)
                act.copy(h2_t, ctx_ps[:, 0:D].rearrange("p (k n) -> p k n", k=DK)).then_inc(h2_copied, 1)

            def gelu(t, half, first):
                act.wait_ge(hidden_ready, 2 * t + half + 1)
                if not first:
                    act.wait_ge(ff_ready, t)
                act.activation(gelu_t[:, 4 * half:4 * half + 4, :].rearrange("p a b -> p (a b)"),
                               score[0][:, half * CH:(half + 1) * CH], ACT.Gelu_apprx_tanh).then_inc(gelu_ready, 1)

            copy_ctxt(0, True)
            copy_h2(0, True)

            def finish(t, first, last):
                gelu(t, 0, first)
                gelu(t, 1, first)
                if not last:
                    copy_ctxt(t + 1, False)
                    copy_h2(t + 1, False)

            finish(0, True, False)
            with act.Fori(1, TILES - 1) as t:
                finish(t, False, False)
            finish(TILES - 1, False, True)


        @block.vector
        def _(dve):
            dve.wait_ge(ident_ready, 1)
            dve.tensor_copy(ident_bf[:, :], ident[:, :]).then_inc(small_step, 1)
            dve.tensor_reduce(head_sel[:, :], ident[:, :].rearrange("p (h t) -> p h t", h=H), AX.X,
                              ALU.add).then_inc(small_step, 1)
            dve.tensor_reduce(quadrant[:, :], ident[:, :].rearrange("p (h t) -> p h t", h=HPG), AX.X,
                              ALU.add).then_inc(small_step, 1)
            dve.wait_ge(small_step, 3)
            dve.tensor_copy(head_block[:, :].rearrange("p (h d) -> p h d", h=H),
                            head_sel[:, :].rearrange("p (h a) -> p h a", a=1).to_broadcast([P, H, HD])).then_inc(
                                small_step, 1)
            dve.wait_ge(ln_loaded, 16 * N_LN)
            dve.tensor_scalar(node[:, :], node_i[:, :], 1.0, None, ALU.is_equal).then_inc(node_ready, 1)
            dve.wait_ge(node_ready, 1)

            def ln1_stats(c, s):
                base = 2 * CT * (2 * c + s)
                dve.wait_ge(x_loaded[s][c % 2], 16 * (c // 2 + 1))
                for i in range(CT):
                    dve.bn_stats(stats[:, s, i, :], h_tok[:, c % 2, s, i, :]).then_inc(stat_step, 1)
                dve.wait_ge(stat_step, base + CT)
                if c > 0:
                    dve.wait_ge(centred, 2 * CT * c)
                for i in range(CT):
                    dve.bn_aggr(moments[:, s, i, :], stats[:, s, i, :]).then_inc(stat_step, 1)
                dve.wait_ge(stat_step, base + 2 * CT)
                dve.tensor_scalar(var_eps[:, s, :], moments[:, s, :, 1], EPS, None, ALU.add).then_inc(var_ready, 1)

            def ln1_centre(c, s):
                dve.wait_ge(rstd_ready, 2 * c + s + 1)
                dve.tensor_tensor(node_rstd[:, s, :], rstd[:, s, :], node[:, CT * c:CT * (c + 1)], ALU.mult).then_inc(
                    stat_done, 1)
                dve.wait_ge(stat_done, 2 * c + s + 1)
                for i in range(CT):
                    row = h_tok[:, c % 2, s, i, :]
                    dve.tensor_scalar(row, row, moments[:, s, i, 0:1], node_rstd[:, s, i:i + 1], ALU.subtract,
                                      ALU.mult).then_inc(centred, 1)

            def ln1_bias_add(c, s):
                dve.wait_ge(scaled, 2 * c + s + 1)
                for i in range(CT):
                    row = h_tok[:, c % 2, s, i, :]
                    dve.scalar_tensor_tensor(out=row, in0=ln1_bc[:, 1, :], scalar=node[:, CT * c + i:CT * c + i + 1],
                                             in1=row, op0=ALU.mult, op1=ALU.add).then_inc(ln1_done, 1)

            def find_edges(t):
                dve.wait_ge(adj_loaded[t % 2], 16 * (t // 2 + 1))
                dve.tensor_scalar(edges[:, t, :], adj_sb[:, t % 2, :], 0.0, None, ALU.not_equal).then_inc(edges_ready, 1)

            def add_kv_bias(t):
                dve.wait_ge(kv_projected, t + 1)
                if t >= CT:
                    dve.wait_ge(mean_summed, t - CT + 1)
                    dve.wait_ge(kv_saved[t % CT], 16 * (t // CT))
                dve.tensor_tensor(kv_out[:, t % CT, :], banks[4 + t % 2], bkv_bc, ALU.add).then_inc(kv_ready, 1)

            for c in range(CHUNKS):
                for s in range(2):
                    ln1_stats(c, s)
                if c == 0:
                    find_edges(0)
                    dve.wait_ge(weights_loaded, 16 * N_WEIGHTS)
                    dve.tensor_scalar(bq_scaled, bq_col, Q_SCALE, None, ALU.mult).then_inc(node_ready, 1)
                    find_edges(1)
                else:
                    for i in range(CT):
                        add_kv_bias(CT * (c - 1) + i)
                        if i % 2 == 1:
                            find_edges(CT * c + i // 2)
                for s in range(2):
                    ln1_centre(c, s)
                if c == 0:
                    dve.wait_ge(iota_ready, 1)
                    dve.tensor_copy(iota[:, :], keys_iota).then_inc(node_ready, 1)
                    dve.wait_ge(const_ready, 2)
                    dve.tensor_reduce(pick_rows[:, 0:UT], ident[:, :].rearrange("p (h t) -> p t h", h=H), AX.X,
                                      ALU.add).then_inc(small_step, 1)
                find_edges(CT * c + 2)
                find_edges(CT * c + 3)
                for s in range(2):
                    ln1_bias_add(c, s)
            for i in range(CT):
                add_kv_bias(CT * (CHUNKS - 1) + i)

            step = 0

            def picked(ins):
                nonlocal step
                step += 1
                return ins.then_inc(pick_step, 1)

            dve.wait_ge(h_turned, 2 * CHUNKS)
            dve.wait_ge(ht_saved, 16 * CHUNKS)
            for g in range(2):
                for n in range(SEGS):
                    dve.wait_ge(coded, SEGS * g + n + 1)
                    dve.scalar_tensor_tensor(out=keys[:, g, n * CH:(n + 1) * CH], in0=banks[(SEGS * g + n) % 2],
                                             scalar=float(N), in1=iota[:, n * CH:(n + 1) * CH], op0=ALU.mult,
                                             op1=ALU.add).then_inc(keys_ready, 1)
                dve.wait_ge(keys_ready, SEGS * (g + 1))
                for r in range(SEG_PICKS // 8):
                    top = [cand[:, g, n, 8 * r:8 * r + 8] for n in range(SEGS)]
                    seg = [keys[:, g, n * CH:(n + 1) * CH] for n in range(SEGS)]
                    for n in range(SEGS):
                        picked(dve.max(top[n], seg[n]))
                    dve.wait_ge(pick_step, step)
                    if 8 * (r + 1) < SEG_PICKS:
                        for n in range(SEGS):
                            picked(dve.match_replace(seg[n], top[n], seg[n], -1.0))
                        dve.wait_ge(pick_step, step)
                picked(dve.tensor_copy(spill[:, g, 0:SEGS], cand[:, g, :, SEG_PICKS - 1]))
                dve.wait_ge(pick_step, step)
                flat = cand[:, g, :, :].rearrange("p a b -> p (a b)")
                for r in range(SLOTS // 8):
                    picked(dve.max(picks[:, g, 8 * r:8 * r + 8], flat))
                    dve.wait_ge(pick_step, step)
                    if r + 1 < SLOTS // 8:
                        picked(dve.match_replace(flat, picks[:, g, 8 * r:8 * r + 8], flat, -1.0))
                        dve.wait_ge(pick_step, step)
                picked(dve.tensor_copy(spill[:, g, SEGS:SEGS + 1], picks[:, g, SLOTS - 1:SLOTS]))
            dve.wait_ge(pick_step, step)
            picked(dve.tensor_reduce(spill_max[:, :], spill[:, :, :], AX.XY, ALU.max))
            assert step == SPILL_STEP
            dve.wait_ge(spill_turned, 1)
            picked(dve.tensor_reduce(spill_all[:, :], banks[2][0:1, 0:P], AX.X, ALU.max))
            dve.wait_ge(pick_step, step)
            dve.tensor_scalar(dense_flag[:, :], spill_all[:, :], float(N), None, ALU.is_ge).then_inc(flag_ready, 1)

            dve.wait_ge(picks_turned, 1)
            picked(dve.tensor_copy(picks_t[:, :], banks[3][:, 0:P]))
            dve.wait_ge(pick_step, step)
            picked(dve.tensor_scalar(source[:, :], picks_t[:, :], N - 1, None, ALU.bitwise_and))
            picked(dve.tensor_scalar(code[:, :], picks_t[:, :], N.bit_length() - 1, None, ALU.logical_shift_right))
            dve.wait_ge(pick_step, step)
            for b in range(G):
                picked(dve.tensor_scalar(bits[:, b, :], code[:, :], b, 1, ALU.logical_shift_right, ALU.bitwise_and))
            dve.wait_ge(pick_step, step)
            dve.wait_ge(mask_cleared, 1)
            for g in range(2):
                rows = slice(SLOTS * g, SLOTS * (g + 1))
                picked(dve.tensor_scalar(slot_mask[rows, :, G * g:G * (g + 1)], bits[rows, :, :].rearrange("p b u -> p u b"),
                                         -NEG, NEG, ALU.mult, ALU.add))
            dve.wait_ge(mean_summed, TILES)
            picked(dve.tensor_copy(mean_v[:, :], banks[7][:, 0:D]))
            dve.wait_ge(degree_ready, TILES)
            picked(dve.tensor_scalar(empty[:, :], degree[:, :], 0.0, None, ALU.is_equal))
            dve.wait_ge(pick_step, step)
            dve.sem_inc(picks_ready, 1)

            flag = read_flag(dve)
            with dve.If(flag == 0):
                def row_maxima(t, v):
                    u, h = t * UPT + v, v % UPT
                    dve.wait_ge(scored, u + 1)
                    dve.tensor_reduce(row_max[:, h:h + 1], s_ps[v % 2][:, 0:P], AX.X, ALU.max).then_inc(max_done, 1)
                    dve.wait_ge(max_done, u + 1)
                    dve.tensor_scalar(neg_max[:, h:h + 1], row_max[:, h:h + 1], NO_EDGE, -1.0, ALU.max,
                                      ALU.mult).then_inc(neg_done, 1)

                def copy_p(t, v):
                    u = t * UPT + v
                    dve.wait_ge(p_turned, u + 1)
                    if not (is_first(t) and v < 2):
                        dve.wait_ge(weighed, u - 1)
                    dve.tensor_copy(prob_t[:, v % 2, :], p_ps[:, 0:P]).then_inc(p_copied, 1)

                def normalise(t, v):
                    u, h = t * UPT + v, v % UPT
                    dve.tensor_scalar(row_sum_up[:, h:h + 1], row_sum[:, h:h + 1], TINY, None, ALU.max).then_inc(
                        norm_step, 1)
                    dve.wait_ge(norm_step, 2 * u + 1)
                    dve.reciprocal(row_recip[:, h:h + 1], row_sum_up[:, h:h + 1]).then_inc(norm_step, 1)
                    if v % SEL == 0 and not is_first(t):
                        dve.wait_ge(selected, 2 * (t - 1) + v // SEL + 1)
                    dve.wait_ge(norm_step, 2 * u + 2)
                    dve.wait_ge(weighed, u + 1)
                    dve.scalar_tensor_tensor(out=weighed_sb[:, h, :], in0=o_ps[v % 2][:, 0:D], scalar=row_recip[:, h:h + 1],
                                             in1=head_block[:, :], op0=ALU.mult, op1=ALU.mult).then_inc(o_ready, 1)

                def sparse(t):
                    for h in range(UPT):
                        copy_p(t, h)
                        if h > 0:
                            normalise(t, h - 1)
                        elif not is_first(t):
                            normalise(t - 1, UPT - 1)
                        if not (is_last(t) and h + 2 >= UPT):
                            row_maxima(t + (h + 2) // UPT, (h + 2) % UPT)

                row_maxima(0, 0)
                row_maxima(0, 1)
                tiles_loop(dve, sparse)
                normalise(TILES - 1, UPT - 1)
                dve.wait_ge(o_ready, UNITS)
                dve.sem_inc(path_done, 1)
            with dve.Else():
                def make_mask(t, first):
                    dve.wait_ge(adj_again, 16 * (t + 1))
                    if not first:
                        dve.wait_ge(masked, 2 * t * H)
                    dve.tensor_scalar(mask_sb[:, :], adj_sb[:, 0, :], 0.0, NEG, ALU.is_equal, ALU.mult).then_inc(mask_ready, 1)
                    dve.wait_ge(mask_ready, t + 1)

                def mask_half(t, h, half, free):
                    u = t * H + h
                    if half == 0 and not free:
                        dve.wait_ge(quarter_turned, QUARTERS * (u - LR + 1))
                    if half == 1:
                        dve.wait_ge(masked, 2 * u + 1)
                    wait_alone(dve, scores_ready, 2 * u + half + 1)
                    start = LOWEST if half == 0 else rowmax[:, h, 0:1]
                    dve.tensor_tensor_reduce(logits[:, h % LR, half * HALF:(half + 1) * HALF], score[half][:, :],
                                             mask_sb[:, half * HALF:(half + 1) * HALF], 1.0, start, ALU.add, ALU.max,
                                             rowmax[:, h, half:half + 1]).then_inc(masked, 1)

                def negate(t, h):
                    dve.wait_ge(masked, 2 * (t * H + h) + 2)
                    dve.tensor_scalar(negmax[:, h:h + 1], rowmax[:, h, 1:2], -1.0, None, ALU.mult).then_inc(negmax_ready, 1)

                def copy_quarter(t, h, q, free):
                    u = t * H + h
                    dve.wait_ge(quarter_turned, QUARTERS * u + q + 1)
                    if q == 1 and not free:
                        dve.wait_ge(ctx_done, u - 1)
                    dve.tensor_copy(probs_t[:, h % 2, 4 * q:4 * q + 4, :].rearrange("p a b -> p (a b)"),
                                    turned[q % 2][:, :]).then_inc(copied_dve, 1)

                def normalise(n, g, saved):
                    if saved is not None:
                        dve.wait_ge(ctx_saved, saved)
                    dve.wait_ge(ctx_back, n + 1)
                    dve.tensor_reduce(ctx_sum[:, :, :], back_ps[:, :].rearrange("p (h j d) -> p h d j", h=HPG, j=HPG), AX.X,
                                      ALU.add).then_inc(ctx_step, 1)
                    dve.reciprocal(recip[:, :], sums[:, g * HPG:(g + 1) * HPG]).then_inc(ctx_step, 1)
                    dve.wait_ge(ctx_step, 2 * n + 2)
                    for i in range(HPG):
                        last = dve.tensor_scalar(ctx_norm[:, (g * HPG + i) * HD:(g * HPG + i + 1) * HD], ctx_sum[:, i, :],
                                                 recip[:, i:i + 1], None, ALU.mult)
                    last.then_inc(ctx_ready, 1)

                def attend(t):
                    first = isinstance(t, int) and t == 0
                    last = isinstance(t, int) and t == TILES - 1
                    for h in range(H):
                        hm, tm = (h + 2) % H, t + (h + 2) // H
                        more = not (last and h + 2 >= H)
                        free = first and h + 2 < LR
                        if more:
                            if hm == 0:
                                make_mask(tm, False)
                            mask_half(tm, hm, 0, free)
                        copy_quarter(t, h, 1, first and h < 2)
                        if more:
                            mask_half(tm, hm, 1, free)
                            negate(tm, hm)
                        copy_quarter(t, h, 3, True)
                        if h == 5:
                            normalise(GROUPS * t, 0, None if first else 16 * t)
                        if h == 1 and not first:
                            normalise(GROUPS * t - 1, 1, None)

                make_mask(0, True)
                for h in range(2):
                    for half in range(2):
                        mask_half(0, h, half, True)
                    negate(0, h)
                attend(0)
                with dve.Fori(1, TILES - 1) as t:
                    attend(t)
                attend(TILES - 1)
                normalise(GROUPS * TILES - 1, 1, None)
                dve.wait_ge(ctx_ready, GROUPS * TILES)
                dve.memset(empty[:, :], 0.0).then_inc(empty_ready, 1)
                dve.wait_ge(empty_ready, 1)
                dve.sem_inc(path_done, 1)

            dve.wait_ge(path_done, ENGINES)
            dve.wait_ge(weights3_loaded, 16 * N_WEIGHTS3)

            def fill_ctx(t, r, n):
                dve.wait_ge(rows_loaded[r], 48 * n)
                dve.scalar_tensor_tensor(out=in3[:, r, 0, :], in0=mean_v[:, :], scalar=empty[:, ds(t, 1)],
                                         in1=in3[:, r, 0, :], op0=ALU.mult, op1=ALU.add).then_inc(ctx_filled, 1)

            def row_stats(src, slot, step, base):
                dve.wait_ge(step, base)
                dve.bn_stats(stats[:, slot, 0, :], src).then_inc(step, 1)
                wait_alone(dve, step, base + 1)
                dve.bn_aggr(moments[:, slot, 0, :], stats[:, slot, 0, :]).then_inc(step, 1)
                dve.wait_ge(step, base + 2)
                dve.tensor_scalar(var_eps[:, slot, 0:1], moments[:, slot, 0, 1:2], EPS, None, ALU.add).then_inc(step, 1)

            def ln2(t, r, first):
                base = 8 * t
                m = node[:, ds(t, 1)]
                dve.wait_ge(attn_ready, t + 1)
                if not first:
                    dve.wait_ge(ln2_step, base)
                dve.tensor_tensor(res, turned[1][:, 0:D], bo_bc, ALU.add).then_inc(ln2_step, 1)
                dve.wait_ge(ln2_step, base + 1)
                dve.scalar_tensor_tensor(out=res, in0=res, scalar=m, in1=in3[:, r, 1, :], op0=ALU.mult,
                                         op1=ALU.add).then_inc(ln2_step, 1)
                row_stats(res, 0, ln2_step, base + 2)
                dve.wait_ge(rstd2_ready, t + 1)
                dve.tensor_scalar(res, res, moments[:, 0, 0, 0:1], rstd[:, 0, 0:1], ALU.subtract,
                                  ALU.mult).then_inc(ln2_step, 1)
                dve.wait_ge(ln2_step, base + 6)
                dve.scalar_tensor_tensor(out=res, in0=res, scalar=m, in1=scale2_bc, op0=ALU.mult,
                                         op1=ALU.mult).then_inc(ln2_step, 1)
                dve.wait_ge(ln2_step, base + 7)
                dve.scalar_tensor_tensor(out=h2[:, r, :], in0=bias2_bc, scalar=m, in1=res, op0=ALU.mult,
                                         op1=ALU.add).then_inc(ln2_step, 1)

            def ln3(t, r, n):
                base = 6 * t
                dve.wait_ge(ff_ready, t + 1)
                if not (isinstance(t, int) and t == 0):
                    dve.wait_ge(ln3_step, base)
                dve.tensor_tensor(res2, back_ps[:, 0:D], h2[:, r, :], ALU.add).then_inc(ln3_step, 1)
                dve.wait_ge(ln3_step, base + 1)
                dve.tensor_tensor(res2, res2, in3[:, r, 2, :], ALU.add).then_inc(ln3_step, 1)
                row_stats(res2, 1, ln3_step, base + 2)
                dve.wait_ge(rstd3_ready, t + 1)
                if n is not None:
                    dve.wait_ge(y_saved[r], 16 * n)
                dve.tensor_scalar(y_out[:, r, :], res2, moments[:, 1, 0, 0:1], rstd[:, 1, 0:1], ALU.subtract,
                                  ALU.mult).then_inc(ln3_step, 1)

            fill_ctx(0, 0, 1)
            ln2(0, 0, True)
            fill_ctx(1, 1, 1)

            def finish(i, last):
                first = isinstance(i, int) and i == 0
                for r in range(2):
                    t = 2 * i + r
                    if not (last and r == 1):
                        ln2(t + 1, 1 - r, False)
                    ln3(t, r, None if first else i)
                    if not last:
                        fill_ctx(t + 2, r, i + 2)

            finish(0, False)
            with dve.Fori(1, TILES // 2 - 1) as i:
                finish(i, False)
            finish(TILES // 2 - 1, True)


_INS = ["x", "adj", "nodemask", "L0_gnn_h_target", "L0_gnn_ln1_scale", "L0_gnn_ln1_bias", "L0_gnn_Wq", "L0_gnn_bq",
        "L0_gnn_Wk", "L0_gnn_bk", "L0_gnn_Wv", "L0_gnn_bv", "L0_gnn_Wo", "L0_gnn_bo", "L0_gnn_ln2_scale",
        "L0_gnn_ln2_bias", "L0_gnn_W1", "L0_gnn_W2"]


def kernel(**inputs):
    import numpy as _np
    import concourse.bacc as _bacc
    from concourse import mybir as _mybir
    from concourse.bass_utils import run_bass_kernel_spmd as _run

    nc = _bacc.Bacc("TRN2", target_bir_lowering=False, num_devices=1)
    arrays, args = {}, []
    for name in _INS:
        a = _np.ascontiguousarray(inputs[name])
        arrays[f"in_{name}_dram"] = a
        args.append(nc.dram_tensor(f"in_{name}_dram", a.shape, _mybir.dt.from_np(a.dtype), kind="ExternalInput").ap())
    shape = inputs["x"].shape
    args.append(nc.dram_tensor("out_0_dram", shape, _mybir.dt.float32, kind="ExternalOutput").ap())
    graph_attention(nc, *args)
    r = _run(nc, [arrays], core_ids=[0])
    return r.results[0]["out_0_dram"]
```

```python
from contextlib import ExitStack

import concourse.bass as bass
from concourse import mybir

ALU = mybir.AluOpType
ACT = mybir.ActivationFunctionType
AX = mybir.AxisListType
F32 = mybir.dt.float32
BF16 = mybir.dt.bfloat16
I32 = mybir.dt.int32
U32 = mybir.dt.uint32

P = 128
EPS = 1e-5
NEG = -1e30
NO_EDGE = -1e29
TINY = 1e-30
LOWEST = -3.0e38
ds = bass.ds


def graph_attention(nc, x, adj, nodemask, h_target, ln1_scale, ln1_bias, Wq, bq, Wk, bk, Wv, bv, Wo, bo,
                    ln2_scale, ln2_bias, W1, W2, out):
    N, D = x.shape
    H = 8
    HD = D // H
    DF = W1.shape[1]
    TILES = N // P
    DK = D // P
    FK = DF // P
    CH = 512
    CT = CH // P
    CHUNKS = N // CH
    Q_SCALE = 1.0 / float(HD) ** 0.5
    G = 8
    UT = 2 * G
    UNITS = N // UT
    UPT = P // UT
    SLOTS = P // 2
    CODE_BANKS = N // CH
    CW = 32
    TPC = CW // UPT
    SEG = 256
    SEGS = N // SEG
    SEG_PICKS = 16
    CAND = SEGS * SEG_PICKS
    KV = 2 * D
    FILL = 4
    US = 2 * UPT
    STEPS = UNITS // US
    RING = 4
    HT = H // DK * UT
    HALF = N // 2
    HPG = 4
    GROUPS = H // HPG
    QUARTERS = 4
    LR = 4
    DENSE_UNITS = TILES * H
    FR = 4

    ctx = ExitStack()
    with ctx:
        def sb(name, shape, dt=F32):
            return ctx.enter_context(nc.sbuf_tensor(name, shape, dt))

        def sem(name):
            return ctx.enter_context(nc.semaphore(name))

        ht_dram = nc.dram_tensor("ht_scratch", (N, D), F32).ap()
        kv_dram = nc.dram_tensor("kv_scratch", (N, KV), F32).ap()
        ctx_dram = nc.dram_tensor("ctx_scratch", (N, D), F32).ap()

        ident = sb("ident", [P, P])
        ident_bf = sb("ident_bf", [P, P], BF16)
        iota = sb("iota", [P, N])
        minus_half = sb("minus_half", [P, CT])
        mean_ones = sb("mean_ones", [P, P])
        code_weights = sb("code_weights", [P, 2, 2 * CW - UPT], BF16)
        quadrant = sb("quadrant", [P, HPG])
        node_i = sb("node_i", [P, TILES], I32)
        node = sb("node", [P, TILES])
        degree = sb("degree", [P, TILES])
        empty = sb("empty", [P, TILES])
        mean_v = sb("mean_v", [P, D])
        mean_vt = sb("mean_vt", [P, DK, P])
        mean_out = sb("mean_out", [P, D])
        q_t = sb("q_t", [P, DK, N])
        mask_sb = sb("mask_sb", [P, N], BF16)
        adj_sb = sb("adj_sb", [P, 2, N], I32)
        stats = sb("stats", [P, 2, CT, 6])
        moments = sb("moments", [P, 2, CT, 2])
        var_eps = sb("var_eps", [P, 2, CT])
        rstd = sb("rstd", [P, 2, CT])
        ln1_col = sb("ln1_col", [P, 2, DK])

        h_tok = sb("h_tok", [P, 2, 2, CT, D])
        keys = h_tok[:, :, :, :, :].rearrange("p r s c d -> p r (s c d)")
        cand = sb("cand", [P, 2, SEGS, SEG_PICKS])
        picks = sb("picks", [P, 2, SLOTS])
        spill = sb("spill", [P, 2, SEGS + 1])
        spill_max = sb("spill_max", [P, 1])
        spill_all = sb("spill_all", [1, 1])
        dense_flag = sb("dense_flag", [1, 1], I32)
        picks_t = sb("picks_t", [P, UNITS], I32)
        source = sb("source", [P, UNITS], I32)
        code = sb("code", [P, UNITS], I32)
        bits = sb("bits", [P, G, UNITS], I32)
        keys_iota = q_t[:, 0, :].bitcast(I32)
        slot_mask = sb("slot_mask", [P, UNITS, UT], BF16)

        arena = sb("arena", [P, 8 * N])
        work = sb("work", [P, 4 * N])
        edges = arena[:, :].bitcast(BF16).rearrange("p (t n) -> p t n", t=TILES)
        h_feat = work[:, 0:2 * DK * CH].rearrange("p (s k n) -> p s k n", s=2, k=DK)
        at = 2 * DK * CH
        wkv = work[:, at:at + DK * KV].rearrange("p (k n) -> p k n", k=DK)
        at += DK * KV
        wq_sb = work[:, at:at + DK * D].rearrange("p (k n) -> p k n", k=DK)
        at += DK * D
        ln1_bc = work[:, at:at + 2 * D].rearrange("p (w n) -> p w n", w=2)
        at += 2 * D
        bkv_bc = work[:, at:at + KV]
        at += KV
        kv_out = work[:, at:at + CT * KV].rearrange("p (r n) -> p r n", r=CT)
        at += CT * KV
        bq_col = work[:, at:at + DK]
        bq_scaled = work[:, at + DK:at + 2 * DK]
        kv_ring = arena[:, 0:US * KV].rearrange("p (r n) -> p r n", r=US)
        at = US * KV
        k_t = arena[:, at:at + RING * D].rearrange("p (r k n) -> p r k n", r=RING, k=DK)
        at += RING * D
        prob = arena[:, at:at + RING * P].rearrange("p (r n) -> p r n", r=RING)
        at += RING * P
        prob_t = arena[:, at:at + RING * P].rearrange("p (r n) -> p r n", r=RING)
        q_blocks = sb("q_blocks", [P, DK, 2 * FILL, HT])
        mask_rows = sb("mask_rows", [P, 2 * FILL, H, UT], BF16)
        source_ring = sb("source_ring", [P, US], U32)
        row_max = sb("row_max", [P, US])
        neg_max = sb("neg_max", [P, US])
        row_sum = sb("row_sum", [P, US])
        row_sum_up = sb("row_sum_up", [P, US])
        row_recip = sb("row_recip", [P, US])
        logits = arena[:, 0:LR * N].rearrange("p (r n) -> p r n", r=LR)
        probs_t = arena[:, LR * N:(LR + 2) * N].rearrange("p (r s n) -> p r s n", r=2, s=TILES)
        k_rows = arena[:, LR * N:(LR + 2) * N].rearrange("p (t n) -> p t n", t=TILES)
        ctx_rows = k_rows
        v_all = arena[:, (LR + 2) * N:(LR + 4) * N].rearrange("p (t n) -> p t n", t=TILES)
        kt_all = work[:, 0:DK * N].rearrange("p (k n) -> p k n", k=DK)
        q_tile = work[:, DK * N:DK * N + DK * P].rearrange("p (k n) -> p k n", k=DK)
        rowmax = sb("rowmax", [P, H, 2])
        negmax = sb("negmax", [P, H])
        sums = sb("sums", [P, H])
        recip = sb("recip", [P, HPG])
        ctx_part = sb("ctx_part", [P, HPG * P])
        ctx_sum = sb("ctx_sum", [P, HPG, HD])
        ctx_norm = sb("ctx_norm", [P, D])
        w1_sb = sb("w1_sb", [P, DK, DF])
        w2_sb = sb("w2_sb", [P, FK, D])
        wo_sb = sb("wo_sb", [P, DK, D])
        fin_bc = sb("fin_bc", [P, 3, D])
        bo_bc, scale2_bc, bias2_bc = (fin_bc[:, w, :] for w in range(3))
        gelu_t = arena[:, 0:FK * P].rearrange("p (k n) -> p k n", k=FK)
        at = FK * P
        ctx_t = arena[:, at:at + D].rearrange("p (k n) -> p k n", k=DK)
        at += D
        h2_t = arena[:, at:at + 2 * D].rearrange("p (r k n) -> p r k n", r=2, k=DK)
        at += 2 * D
        rows_in = arena[:, at:at + FR * 2 * D].rearrange("p (r w n) -> p r w n", r=FR, w=2)
        at += FR * 2 * D
        bias_row = arena[:, at:at + 2 * D].rearrange("p (r n) -> p r n", r=2)
        at += 2 * D
        h2 = arena[:, at:at + 2 * D].rearrange("p (r n) -> p r n", r=2)
        at += 2 * D
        res = arena[:, at:at + D]
        res2 = arena[:, at + D:at + 2 * D]
        at += 2 * D
        y_out = arena[:, at:at + 2 * D].rearrange("p (r n) -> p r n", r=2)

        bank = [ctx.enter_context(nc.psum_tensor(f"bank{i}", [P, CH], F32)) for i in range(4)]
        score = [ctx.enter_context(nc.psum_tensor(f"score{i}", [P, HALF], F32)) for i in range(2)]
        banks = [b[:, :] for b in bank] + [score[i][:, j * CH:(j + 1) * CH] for i in range(2) for j in range(2)]
        k_ps, p_ps, s_ps, o_ps = banks[0], banks[1], banks[2:6], banks[6:8]
        turned = bank[0:2]
        ctx_ps = bank[2]
        back_ps = bank[3]

        def dram_tiles(a):
            return a.rearrange("(c t p) d -> p c t d", p=P, t=CT)

        ln_loaded = sem("ln_loaded")
        weights_loaded = sem("weights_loaded")
        x_loaded = [[sem(f"x_loaded{s}{r}") for r in range(2)] for s in range(2)]
        adj_loaded = [sem(f"adj_loaded{r}") for r in range(2)]
        const_step = sem("const_step")
        ident_ready = sem("ident_ready")
        const_ready = sem("const_ready")
        iota_ready = sem("iota_ready")
        small_step = sem("small_step")
        node_ready = sem("node_ready")
        stat_step = sem("stat_step")
        var_ready = sem("var_ready")
        rstd_ready = sem("rstd_ready")
        ln1_done = sem("ln1_done")
        ht_saved = sem("ht_saved")
        scaled = sem("scaled")
        ht_ready = sem("ht_ready")
        edges_ready = sem("edges_ready")
        degree_ready = sem("degree_ready")
        h_turned = sem("h_turned")
        h_copied = sem("h_copied")
        kv_projected = sem("kv_projected")
        kv_ready = sem("kv_ready")
        kv_saved = [sem(f"kv_saved{r}") for r in range(CT)]
        mean_summed = sem("mean_summed")
        q_projected = sem("q_projected")
        q_copied = sem("q_copied")
        coded = sem("coded")
        keys_ready = sem("keys_ready")
        pick_step = sem("pick_step")
        spill_turned = sem("spill_turned")
        flag_ready = sem("flag_ready")
        picks_turned = sem("picks_turned")
        mask_cleared = sem("mask_cleared")
        picks_ready = sem("picks_ready")
        source_ready = sem("source_ready")
        q_blocks_ready = sem("q_blocks_ready")
        mask_rows_ready = sem("mask_rows_ready")
        gathered = [sem(f"gathered{r}") for r in range(US)]
        k_turned = sem("k_turned")
        k_copied = sem("k_copied")
        scored = sem("scored")
        max_done = sem("max_done")
        neg_done = sem("neg_done")
        exp_done = sem("exp_done")
        norm_step = sem("norm_step")
        p_turned = sem("p_turned")
        p_copied = sem("p_copied")
        weighed = sem("weighed")
        o_copied = sem("o_copied")
        rows_ready = sem("rows_ready")
        kt_turned = sem("kt_turned")
        kt_copied = sem("kt_copied")
        adj_again = sem("adj_again")
        mask_ready = sem("mask_ready")
        q_stacked = [sem(f"q_stacked{g}") for g in range(GROUPS)]
        scores_ready = sem("scores_ready")
        masked = sem("masked")
        negmax_ready = sem("negmax_ready")
        probs_ready = sem("probs_ready")
        quarter_turned = sem("quarter_turned")
        copied_act = sem("copied_act")
        copied_dve = sem("copied_dve")
        ctx_done = sem("ctx_done")
        ctx_copied = sem("ctx_copied")
        ctx_back = sem("ctx_back")
        ctx_step = sem("ctx_step")
        ctx_ready = sem("ctx_ready")
        ctx_saved = sem("ctx_saved")
        ctx_rows_ready = sem("ctx_rows_ready")
        ctxt_back = sem("ctxt_back")
        ctxt_kept = sem("ctxt_kept")
        path_done = sem("path_done")
        weights3_loaded = sem("weights3_loaded")
        rows_loaded = [sem(f"rows_loaded{r}") for r in range(FR)]
        empty_ready = sem("empty_ready")
        mean_ready = sem("mean_ready")
        mean_turned = sem("mean_turned")
        mean_copied = sem("mean_copied")
        mean_projected = sem("mean_projected")
        bias_ready = sem("bias_ready")
        ctxt_copied = sem("ctxt_copied")
        attn_ready = sem("attn_ready")
        ln2_step = sem("ln2_step")
        rstd2_ready = sem("rstd2_ready")
        rstd3_ready = sem("rstd3_ready")
        h2_turned = sem("h2_turned")
        h2_copied = sem("h2_copied")
        hidden_ready = sem("hidden_ready")
        gelu_ready = sem("gelu_ready")
        ff_ready = sem("ff_ready")
        ln3_step = sem("ln3_step")
        y_saved = [sem(f"y_saved{r}") for r in range(2)]
        lone_waits = {eng.engine: sem(f"lone_waits_{n}") for n, eng in (("sp", nc.sync), ("dve", nc.vector), ("pool", nc.gpsimd))}

        block = ctx.enter_context(nc.Block())
        N_LN = 5
        N_WEIGHTS = 7
        N_WEIGHTS3 = 6
        ENGINES = 5
        ROUNDS = SEG_PICKS // 8
        SPILL_STEP = 2 * (SEGS * (2 * ROUNDS - 1) + 2 * (SLOTS // 8) - 1 + 2) + 1
        KEYS = 2 * CODE_BANKS

        def wait_alone(eng, semaphore, value):
            eng.wait_ge(semaphore, value)
            eng.sem_inc(lone_waits[eng.engine], 1)

        def is_first(t):
            return isinstance(t, int) and t == 0

        def is_last(t):
            return isinstance(t, int) and t == TILES - 1

        def read_flag(eng):
            eng.wait_ge(flag_ready, 1)
            return eng.value_load(dense_flag[0:1, 0:1], min_val=0, max_val=1)

        def ends(s):
            return isinstance(s, int) and s == STEPS - 1

        def steps_loop(eng, body):
            body(0)
            with eng.Fori(1, STEPS - 1) as s:
                body(s)
            body(STEPS - 1)

        @block.sync
        def _(sp):
            def load_x(s, c):
                src = dram_tiles(x if s == 0 else h_target)
                sp.dma_start(h_tok[:, c % 2, s, :, :], src[:, c, :, :]).then_inc(x_loaded[s][c % 2], 16)

            def load_adj(t):
                sp.dma_start(adj_sb[:, t % 2, :], adj[t * P:(t + 1) * P, :]).then_inc(adj_loaded[t % 2], 16)

            def load_w(dst, a):
                sp.dma_start(dst, a.rearrange("(k p) n -> p k n", p=P)).then_inc(weights_loaded, 16)

            for s in range(2):
                load_x(s, 0)
            load_adj(0)
            sp.dma_start(node_i[:, :], nodemask.rearrange("(t p) -> p t", p=P),
                         allow_slow_non_contiguous=True).then_inc(ln_loaded, 16)
            for w, a in enumerate((ln1_scale, ln1_bias)):
                sp.dma_start(ln1_bc[:, w, :], a.partition_broadcast(P)).then_inc(ln_loaded, 16)
                sp.dma_start(ln1_col[:, w, :], a.rearrange("(k p) -> p k", p=P),
                             allow_slow_non_contiguous=True).then_inc(ln_loaded, 16)
            load_w(wkv[:, :, 0:D], Wk)
            load_w(wkv[:, :, D:KV], Wv)
            for s in range(2):
                load_x(s, 1)
            load_w(wq_sb, Wq)
            load_adj(1)
            sp.dma_start(bkv_bc[:, 0:D], bk.partition_broadcast(P)).then_inc(weights_loaded, 16)
            sp.dma_start(bkv_bc[:, D:KV], bv.partition_broadcast(P)).then_inc(weights_loaded, 16)
            sp.dma_start(bq_col, bq.rearrange("(k p) -> p k", p=P),
                         allow_slow_non_contiguous=True).then_inc(weights_loaded, 16)
            sp.dma_start(fin_bc[:, 0, :], bo.partition_broadcast(P)).then_inc(weights_loaded, 16)

            def save_kv(c):
                for i in range(CT):
                    t = CT * c + i
                    sp.wait_ge(kv_ready, t + 1)
                    sp.dma_start(kv_dram[t * P:(t + 1) * P, :], kv_out[:, i, :]).then_inc(kv_saved[i], 16)

            def next_adj(t):
                if t < TILES:
                    sp.wait_ge(edges_ready, t - 1)
                    load_adj(t)

            for c in range(CHUNKS):
                if c > 0:
                    save_kv(c - 1)
                next_adj(CT * c + 2)
                next_adj(CT * c + 3)
                if c + 2 < CHUNKS:
                    sp.wait_ge(h_turned, 2 * c + 1)
                    load_x(0, c + 2)
                next_adj(CT * c + 4)
                next_adj(CT * c + 5)
                if c + 2 < CHUNKS:
                    sp.wait_ge(ht_saved, 16 * (c + 1))
                    load_x(1, c + 2)
            save_kv(CHUNKS - 1)
            for dst, a in ((w1_sb, W1), (w2_sb, W2), (wo_sb, Wo)):
                sp.dma_start(dst[:, :, :], a.rearrange("(k p) n -> p k n", p=P)).then_inc(weights3_loaded, 16)
            for w, a in enumerate((bo, ln2_scale, ln2_bias)):
                if w == 0:
                    sp.wait_ge(weights_loaded, 16 * N_WEIGHTS)
                sp.dma_start(fin_bc[:, w, :], a.partition_broadcast(P)).then_inc(weights3_loaded, 16)

            flag = read_flag(sp)
            with sp.If(flag == 0):
                sp.sem_inc(path_done, 1)
            with sp.Else():
                for r in range(CT):
                    sp.wait_ge(kv_saved[r], 16 * CHUNKS)
                sp.wait_ge(coded, KEYS)
                sp.wait_ge(degree_ready, TILES)
                kv_rows = kv_dram.rearrange("(t p) n -> p t n", p=P)
                sp.dma_start(k_rows, kv_rows[:, :, 0:D]).then_inc(rows_ready, 16)
                sp.dma_start(v_all, kv_rows[:, :, D:KV]).then_inc(rows_ready, 16)
                sp.dma_start(adj_sb[:, 0, :], adj[0:P, :]).then_inc(adj_again, 16)
                sp.wait_ge(kv_projected, TILES)
                sp.wait_ge(q_copied, DK * CHUNKS)

                def load_q(t, g):
                    sp.dma_start(q_tile[:, g, :], q_t[:, g, ds(t * P, P)]).then_inc(q_stacked[g], 16)

                for g in range(GROUPS):
                    load_q(0, g)

                def attend(t):
                    if not is_last(t):
                        wait_alone(sp, mask_ready, t + 1)
                        sp.dma_start(adj_sb[:, 0, :], adj[ds((t + 1) * P, P), :]).then_inc(adj_again, 16)
                        for g in range(GROUPS):
                            wait_alone(sp, scores_ready, 2 * (t * H + HPG * (g + 1)))
                            load_q(t + 1, g)
                    wait_alone(sp, ctx_ready, GROUPS * (t + 1))
                    sp.dma_start(ctx_dram[ds(t * P, P), :], ctx_norm[:, :]).then_inc(ctx_saved, 16)

                with sp.Fori(0, TILES - 1) as t:
                    attend(t)
                attend(TILES - 1)
                sp.wait_ge(ctx_saved, 16 * TILES)
                sp.dma_start(ctx_rows, ctx_dram.rearrange("(t p) n -> p t n", p=P)).then_inc(ctx_rows_ready, 16)
                sp.sem_inc(path_done, 1)

            sp.wait_ge(path_done, ENGINES)
            sp.wait_ge(ht_saved, 16 * CHUNKS)

            def load_rows(t, r):
                for w, a in enumerate((ht_dram, x)):
                    sp.dma_start(rows_in[:, r, w, :], a[ds(t * P, P), :]).then_inc(rows_loaded[r], 16)

            def save_rows(t, r):
                wait_alone(sp, ln3_step, 6 * t + 6)
                sp.dma_start(out[ds(t * P, P), :], y_out[:, r, :]).then_inc(y_saved[r], 16)

            for r in range(FR):
                load_rows(r, r)

            def finish(i, last):
                for r in range(FR):
                    save_rows(FR * i + r, r % 2)
                    if not last:
                        load_rows(FR * i + FR + r, r)

            with sp.Fori(0, TILES // FR - 1) as i:
                finish(i, False)
            finish(TILES // FR - 1, True)
            for r in range(2):
                sp.wait_ge(y_saved[r], 16 * (TILES // 2))
            for r in range(CT):
                sp.wait_ge(kv_saved[r], 16 * CHUNKS)

        @block.gpsimd
        def _(pool):
            def select_step(n, out_ap, pattern, base, fill):
                pool.wait_ge(const_step, n)
                pool.affine_select(out=out_ap, in_=out_ap, compare_op=ALU.not_equal, fill=fill, base=base,
                                   pattern=pattern, channel_multiplier=1).then_inc(const_step, 1)

            pool.memset(ident[:, :], 0.0).then_inc(const_step, 1)
            select_step(1, ident[:, :], [[-1, P]], 0, 1.0)
            pool.wait_ge(const_step, 2)
            pool.memset(minus_half[:, :], -0.5).then_inc(ident_ready, 1)
            pool.wait_ge(ident_ready, 1)

            def rsqrt1(n):
                s = n % 2
                pool.wait_ge(var_ready, n + 1)
                pool.tensor_tensor(rstd[:, s, :], var_eps[:, s, :], minus_half[:, :], ALU.pow).then_inc(rstd_ready, 1)

            def scale_targets(c):
                pool.wait_ge(h_turned, 2 * c + 2)
                rows = h_tok[:, c % 2, 1, :, :]
                pool.tensor_tensor(rows, rows, ln1_bc[:, 0:1, :].to_broadcast([P, CT, D]), ALU.mult).then_inc(scaled, 1)
                pool.wait_ge(scaled, c + 1)
                pool.tensor_tensor(rows, rows, ln1_bc[:, 1:2, :].to_broadcast([P, CT, D]), ALU.add).then_inc(ht_ready, 1)
                pool.wait_ge(ht_ready, c + 1)
                pool.dma_start(dram_tiles(ht_dram)[:, c, :, :], rows).then_inc(ht_saved, 16)

            def constants():
                pool.memset(code_weights[:, :, :], 0.0).then_inc(const_step, 1)
                n = 3
                for g in range(2):
                    for b in range(G):
                        select_step(n, code_weights[:, g, CW - UPT:CW], [[-UT, UPT]], -(G * g + b), float(2 ** b))
                        n += 1
                pool.wait_ge(const_step, n)
                pool.memset(slot_mask[:, :, :], NEG).then_inc(mask_cleared, 1)

            pool.iota(keys_iota, pattern=[[1, N]], base=0, channel_multiplier=0).then_inc(iota_ready, 1)
            pool.memset(mean_ones[:, :], 1.0 / N).then_inc(const_ready, 1)
            for s in range(2):
                rsqrt1(s)
            constants()
            for c in range(CHUNKS):
                if c + 1 < CHUNKS:
                    for s in range(2):
                        rsqrt1(2 * (c + 1) + s)
                scale_targets(c)

            flag = read_flag(pool)
            with pool.If(flag == 0):
                pool.wait_ge(picks_ready, 1)
                pool.wait_ge(coded, KEYS)
                for r in range(CT):
                    pool.wait_ge(kv_saved[r], 16 * CHUNKS)

                def sparse(s):
                    for h in range(US):
                        u = s * US + h
                        if h % FILL == 0:
                            if not is_first(s):
                                pool.wait_ge(gathered[h + FILL - 1], 16 * s)
                            pool.tensor_copy(source_ring[:, h:h + FILL],
                                             source[:, ds(u, FILL)].bitcast(U32)).then_inc(source_ready, 1)
                            wait_alone(pool, source_ready, US // FILL * s + h // FILL + 1)
                        if not is_first(s):
                            wait_alone(pool, weighed, u - US + 1)
                        pool.indirect_dma_start(kv_ring[:, h, :], None, kv_dram[:, :],
                                                bass.IndirectOffsetOnAxis(ap=source_ring[:, h:h + 1], axis=0)).then_inc(
                                                    gathered[h], 16)

                steps_loop(pool, sparse)
                pool.sem_inc(path_done, 1)
            with pool.Else():
                pool.sem_inc(path_done, 1)

            pool.wait_ge(path_done, ENGINES)

            def rsqrt2(t):
                pool.wait_ge(ln2_step, 8 * t + 5)
                pool.tensor_tensor(rstd[:, 0, 0:1], var_eps[:, 0, 0:1], minus_half[:, 0:1], ALU.pow).then_inc(rstd2_ready, 1)

            def rsqrt3(t):
                pool.wait_ge(ln3_step, 6 * t + 5)
                pool.tensor_tensor(rstd[:, 1, 0:1], var_eps[:, 1, 0:1], minus_half[:, 0:1], ALU.pow).then_inc(rstd3_ready, 1)

            rsqrt2(0)
            rsqrt2(1)
            with pool.Fori(0, TILES - 2) as t:
                rsqrt2(t + 2)
                rsqrt3(t)
            rsqrt3(TILES - 2)
            rsqrt3(TILES - 1)

        @block.tensor
        def _(pe):
            pe.wait_ge(ident_ready, 1)

            def turn_chunk(c, s):
                pe.wait_ge(ln1_done, CT * (2 * c + s + 1))
                if c > 0:
                    pe.wait_ge(h_copied, DK * (2 * c + s - 1))
                for k in range(DK):
                    for t in range(CT):
                        mm = pe.transpose(banks[2 * s + k][:, t * P:(t + 1) * P],
                                          h_tok[:, c % 2, s, t, k * P:(k + 1) * P], ident[:, :])
                mm.then_inc(h_turned, 1)

            def sum_mean(c):
                for i in range(CT):
                    t = CT * c + i
                    pe.wait_ge(kv_ready, t + 1)
                    pe.matmul(banks[7][:, 0:D], mean_ones[:, :], kv_out[:, i, D:KV], start=(t == 0),
                              stop=(t == TILES - 1)).then_inc(mean_summed, 1)

            def project_kv(c):
                pe.wait_ge(h_copied, DK * (2 * c + 1))
                for i in range(CT):
                    t = CT * c + i
                    if t >= 2:
                        pe.wait_ge(kv_ready, t - 1)
                    for k in range(DK):
                        mm = pe.matmul(banks[4 + t % 2], h_feat[:, 0, k, i * P:(i + 1) * P], wkv[:, k, :],
                                       start=(k == 0), stop=(k == DK - 1))
                    mm.then_inc(kv_projected, 1)

            def project_q(c):
                pe.wait_ge(h_copied, DK * (2 * c + 2))
                for m in range(DK):
                    if c > 0 or m > 0:
                        pe.wait_ge(q_copied, DK * c + m)
                    for k in range(DK):
                        mm = pe.matmul(banks[6], wq_sb[:, k, m * P:(m + 1) * P], h_feat[:, 1, k, :],
                                       start=(k == 0), stop=(k == DK - 1))
                    mm.then_inc(q_projected, 1)

            pe.wait_ge(const_ready, 1)
            turn_chunk(0, 0)
            turn_chunk(0, 1)
            pe.wait_ge(weights_loaded, 16 * N_WEIGHTS)
            for c in range(CHUNKS):
                project_kv(c)
                if c + 1 < CHUNKS:
                    turn_chunk(c + 1, 0)
                project_q(c)
                if c + 1 < CHUNKS:
                    turn_chunk(c + 1, 1)
                sum_mean(c)

            pe.wait_ge(mask_cleared, 1)
            pe.wait_ge(h_copied, 2 * DK * CHUNKS)
            pe.wait_ge(edges_ready, TILES)
            for g in range(2):
                for n in range(CODE_BANKS):
                    i = CODE_BANKS * g + n
                    if i >= 4:
                        pe.wait_ge(keys_ready, i - 3)
                    for j in range(TPC):
                        for q in range(TILES // TPC):
                            t = TPC * q + j
                            at = CW - UPT * (j + 1)
                            mm = pe.matmul(banks[i % 4][CW * q:CW * (q + 1), :], code_weights[:, g, at:at + CW],
                                           edges[:, t, n * CH:(n + 1) * CH], start=(j == 0), stop=(j == TPC - 1),
                                           skip_group_check=True)
                    mm.then_inc(coded, 1)

            pe.wait_ge(mean_ready, 1)
            pe.wait_ge(kv_ready, TILES)
            for k in range(DK):
                mm = pe.transpose(banks[4][:, k * P:(k + 1) * P], mean_v[:, k * P:(k + 1) * P], ident[:, :])
            mm.then_inc(mean_turned, 1)
            pe.wait_ge(mean_copied, 1)
            pe.wait_ge(weights3_loaded, 16 * N_WEIGHTS3)
            for k in range(DK):
                mm = pe.matmul(banks[5][:, 0:D], mean_vt[:, k, :], wo_sb[:, k, :], start=(k == 0), stop=(k == DK - 1))
            mm.then_inc(mean_projected, 1)
            pe.wait_ge(pick_step, SPILL_STEP)
            pe.transpose(banks[2][0:1, 0:P], spill_max[:, :], ident[:, :]).then_inc(spill_turned, 1)
            pe.transpose(banks[3][:, 0:P], picks[:, :, :].rearrange("p g s -> p (g s)"), ident[:, :]).then_inc(
                picks_turned, 1)

            flag = read_flag(pe)
            with pe.If(flag == 0):
                def turn_k(s, v):
                    u, h = s * US + v, v % US
                    pe.wait_ge(gathered[h], 16 * (s + v // US + 1))
                    if not (is_first(s) and v == 0):
                        pe.wait_ge(k_copied, u)
                    for k in range(DK):
                        mm = pe.transpose(k_ps[:, k * P:(k + 1) * P], kv_ring[:, h, k * P:(k + 1) * P], ident[:, :])
                    mm.then_inc(k_turned, 1)

                def scores(s, v):
                    u, h = s * US + v, v % (2 * FILL)
                    if v % FILL == 0:
                        half = US // FILL * s + v // FILL
                        pe.wait_ge(q_blocks_ready, DK * (half + 1))
                        pe.wait_ge(mask_rows_ready, half + 1)
                    pe.wait_ge(k_copied, u + 1)
                    if not (is_first(s) and v < RING):
                        pe.wait_ge(exp_done, u - RING + 1)
                    pe.matmul(s_ps[v % RING][:, 0:P], mask_rows[:, h, :, :].rearrange("p a b -> p (a b)"), ident_bf[:, :],
                              start=True, stop=False, skip_group_check=True)
                    for k in range(DK):
                        mm = pe.matmul(s_ps[v % RING][HT * k:HT * (k + 1), 0:P], q_blocks[:, k, h, :], k_t[:, v % RING, k, :],
                                       start=False, stop=True, skip_group_check=True)
                    mm.then_inc(scored, 1)

                def turn_p(s, v):
                    u = s * US + v
                    pe.wait_ge(norm_step, 3 * (u + 1))
                    if not (is_first(s) and v == 0):
                        pe.wait_ge(p_copied, u)
                    pe.transpose(p_ps[:, 0:P], prob[:, v % RING, :], ident[:, :]).then_inc(p_turned, 1)

                def weigh(s, v):
                    u, h = s * US + v, v % US
                    pe.wait_ge(p_copied, u + 1)
                    if v % UPT == 0 and not (is_first(s) and v < US):
                        pe.wait_ge(o_copied, US // UPT * (s - 1) + v // UPT + 1)
                    for k in range(DK):
                        for q in range(HPG):
                            head = HPG * k + q
                            at = k * P + v % UPT * UT
                            mm = pe.matmul(o_ps[h // UPT][HD * q:HD * (q + 1), at:at + UT],
                                           kv_ring[:, h, D + head * HD:D + (head + 1) * HD],
                                           prob_t[:, v % RING, head * UT:(head + 1) * UT], start=True, stop=True,
                                           skip_group_check=True)
                    mm.then_inc(weighed, 1)

                def sparse(s):
                    for h in range(US):
                        turn_p(s, h)
                        if h > 0:
                            weigh(s, h - 1)
                        elif not is_first(s):
                            weigh(s - 1, US - 1)
                        if not (ends(s) and h + 3 >= US):
                            scores(s + (h + 3) // US, (h + 3) % US)
                        if not (ends(s) and h + 4 >= US):
                            turn_k(s + (h + 4) // US, (h + 4) % US)

                pe.wait_ge(small_step, 2)
                turn_k(0, 0)
                for v in range(3):
                    turn_k(0, v + 1)
                    scores(0, v)
                steps_loop(pe, sparse)
                weigh(STEPS - 1, US - 1)
                pe.wait_ge(weighed, UNITS)
                pe.sem_inc(path_done, 1)
            with pe.Else():
                pe.wait_ge(rows_ready, 32)
                for t in range(TILES):
                    for k in range(DK):
                        if t * DK + k >= 2:
                            pe.wait_ge(kt_copied, t * DK + k - 1)
                        pe.transpose(banks[k][:, 0:P], k_rows[:, t, k * P:(k + 1) * P], ident[:, :]).then_inc(kt_turned, 1)
                pe.wait_ge(kt_copied, DK * TILES)

                def score_half(t, h, half, first):
                    rows = slice(HD * (h % HPG), HD * (h % HPG + 1))
                    if half == 0 and h % HPG == 0:
                        pe.wait_ge(q_stacked[h // HPG], 16 * (t + 1))
                    if not first:
                        pe.wait_ge(masked, 2 * (t * H + h) - 1 + half)
                    for n in range(HALF // CH):
                        col = half * HALF + n * CH
                        mm = pe.matmul(score[half][:, n * CH:(n + 1) * CH], q_tile[rows, h // HPG, :],
                                       kt_all[rows, h // HPG, col:col + CH], start=True, stop=True)
                    mm.then_inc(scores_ready, 1)

                def turn_quarter(t, h, q, first):
                    u = t * H + h
                    if q == 0:
                        pe.wait_ge(probs_ready, u + 1)
                    if not (first and q < 2):
                        pe.wait_ge(copied_act if q % 2 == 0 else copied_dve, 2 * u + q // 2)
                    for i in range(4):
                        b = 4 * q + i
                        mm = pe.transpose(turned[q % 2][:, i * P:(i + 1) * P], logits[:, h % LR, b * P:(b + 1) * P],
                                          ident[:, :])
                    mm.then_inc(quarter_turned, 1)

                def weigh_half(t, h, half, first_tile):
                    u = t * H + h
                    if half == 0:
                        pe.wait_ge(copied_act, 2 * u + 2)
                        pe.wait_ge(copied_dve, 2 * u + 2)
                        if h % HPG == 0 and not (first_tile and h == 0):
                            pe.wait_ge(ctx_copied, GROUPS * t + h // HPG)
                    for k in range(2 * half, 2 * half + 2):
                        for j in range(HPG):
                            s = HPG * k + j
                            mm = pe.matmul(ctx_ps[HD * j:HD * (j + 1), (h % HPG) * P:(h % HPG + 1) * P],
                                           v_all[:, s, h * HD:(h + 1) * HD], probs_t[:, h % 2, s, :],
                                           start=(k == 0), stop=(k == TILES // HPG - 1), skip_group_check=True)
                    if half == 1:
                        mm.then_inc(ctx_done, 1)

                def turn_back(n, first):
                    pe.wait_ge(ctx_copied, n + 1)
                    if not first:
                        pe.wait_ge(ctx_step, 2 * n - 1)
                    for i in range(HPG):
                        mm = pe.transpose(back_ps[:, i * P:(i + 1) * P], ctx_part[:, i * P:(i + 1) * P], ident[:, :])
                    mm.then_inc(ctx_back, 1)

                def attend(t):
                    first = isinstance(t, int) and t == 0
                    last = isinstance(t, int) and t == TILES - 1
                    for h in range(H):
                        hs, ts = (h + 3) % H, t + (h + 3) // H
                        hw, tw = (h - 1) % H, t + (h - 1) // H
                        more = not (last and h + 3 >= H)
                        before = not (first and h == 0)
                        turn_quarter(t, h, 0, first and h == 0)
                        if before:
                            weigh_half(tw, hw, 0, first)
                        turn_quarter(t, h, 1, first and h == 0)
                        if more:
                            score_half(ts, hs, 0, False)
                        turn_quarter(t, h, 2, first and h == 0)
                        if before:
                            weigh_half(tw, hw, 1, first)
                        turn_quarter(t, h, 3, first and h == 0)
                        if more:
                            score_half(ts, hs, 1, False)
                        if h == 5:
                            turn_back(GROUPS * t, first)
                        if h == 1 and not first:
                            turn_back(GROUPS * t - 1, False)

                for h in range(3):
                    for half in range(2):
                        score_half(0, h, half, h == 0)
                attend(0)
                with pe.Fori(1, TILES - 1) as t:
                    attend(t)
                attend(TILES - 1)
                weigh_half(TILES - 1, H - 1, 0, False)
                weigh_half(TILES - 1, H - 1, 1, False)
                turn_back(GROUPS * TILES - 1, False)
                pe.wait_ge(ctx_rows_ready, 16)
                for t in range(TILES):
                    for k in range(DK):
                        if t * DK + k >= 2:
                            pe.wait_ge(ctxt_kept, t * DK + k - 1)
                        pe.transpose(banks[k][:, 0:P], ctx_rows[:, t, k * P:(k + 1) * P], ident[:, :]).then_inc(ctxt_back, 1)
                pe.sem_inc(path_done, 1)

            pe.wait_ge(path_done, ENGINES)
            pe.wait_ge(weights3_loaded, 16 * N_WEIGHTS3)

            def out_project(t):
                pe.wait_ge(ctxt_copied, t + 1)
                if not is_first(t):
                    pe.wait_ge(ln2_step, 8 * t - 7)
                for k in range(DK):
                    mm = pe.matmul(turned[1][:, 0:D], ctx_t[:, k, :], wo_sb[:, k, :], start=(k == 0),
                                   stop=(k == DK - 1))
                mm.then_inc(attn_ready, 1)

            def turn_h2(t, r):
                pe.wait_ge(ln2_step, 8 * t + 8)
                if not is_first(t):
                    pe.wait_ge(h2_copied, t)
                for k in range(DK):
                    mm = pe.transpose(ctx_ps[:, k * P:(k + 1) * P], h2[:, r % 2, k * P:(k + 1) * P], ident[:, :])
                mm.then_inc(h2_turned, 1)

            def mlp_in(t, r):
                pe.wait_ge(h2_copied, t + 1)
                if not is_first(t):
                    pe.wait_ge(gelu_ready, 2 * t)
                for f in range(FK):
                    for k in range(DK):
                        mm = pe.matmul(score[0][:, f * P:(f + 1) * P], w1_sb[:, k, f * P:(f + 1) * P],
                                       h2_t[:, r % 2, k, :], start=(k == 0), stop=(k == DK - 1))
                    if f % 4 == 3:
                        mm.then_inc(hidden_ready, 1)

            def mlp_out(t, half):
                pe.wait_ge(gelu_ready, 2 * t + half + 1)
                if half == 0 and not is_first(t):
                    pe.wait_ge(ln3_step, 6 * t - 5)
                for f in range(FK // 2 * half, FK // 2 * (half + 1)):
                    mm = pe.matmul(back_ps[:, 0:D], gelu_t[:, f, :], w2_sb[:, f, :], start=(f == 0), stop=(f == FK - 1))
                if half == 1:
                    mm.then_inc(ff_ready, 1)

            for t in range(2):
                out_project(t)
            turn_h2(0, 0)

            def finish(i, last):
                for r in range(FR):
                    t = FR * i + r
                    mlp_in(t, r)
                    if not (last and r + 1 >= FR):
                        turn_h2(t + 1, r + 1)
                    mlp_out(t, 0)
                    if not (last and r + 2 >= FR):
                        out_project(t + 2)
                    mlp_out(t, 1)

            finish(0, False)
            with pe.Fori(1, TILES // FR - 1) as i:
                finish(i, False)
            finish(TILES // FR - 1, True)


        @block.scalar
        def _(act):
            def copy_chunk(c, s):
                act.wait_ge(h_turned, 2 * c + s + 1)
                if c > 0:
                    act.wait_ge(kv_projected if s == 0 else q_projected, (CT if s == 0 else DK) * c)
                for k in range(DK):
                    act.activation(h_feat[:, s, k, :], banks[2 * s + k], ACT.Identity, bias=ln1_col[:, 1, k:k + 1],
                                   scale=ln1_col[:, 0, k:k + 1]).then_inc(h_copied, 1)

            def count_edges(t):
                act.wait_ge(edges_ready, t + 1)
                if t > 0:
                    act.wait_ge(degree_ready, t)
                act.activation(mask_sb[:, :], edges[:, t, :], ACT.Identity, bias=0.0, scale=1.0,
                               accum_out=degree[:, t:t + 1]).then_inc(degree_ready, 1)

            def copy_q(c):
                for m in range(DK):
                    act.wait_ge(q_projected, DK * c + m + 1)
                    act.activation(q_t[:, m, c * CH:(c + 1) * CH], banks[6], ACT.Identity, bias=bq_scaled[:, m:m + 1],
                                   scale=Q_SCALE).then_inc(q_copied, 1)

            act.wait_ge(node_ready, 3)
            copy_chunk(0, 0)
            copy_chunk(0, 1)
            for c in range(CHUNKS):
                if c > 0:
                    for i in range(2):
                        count_edges(CT * c - 2 + i)
                if c + 1 < CHUNKS:
                    copy_chunk(c + 1, 0)
                copy_q(c)
                if c + 1 < CHUNKS:
                    copy_chunk(c + 1, 1)
                for i in range(2):
                    count_edges(CT * c + i)
            for i in range(2):
                count_edges(TILES - 2 + i)

            act.wait_ge(mean_turned, 1)
            act.copy(mean_vt[:, :, :], banks[4][:, 0:D].rearrange("p (k n) -> p k n", k=DK)).then_inc(mean_copied, 1)

            flag = read_flag(act)
            with act.If(flag == 0):
                def spread_mask(half, slot, first):
                    if not first:
                        act.wait_ge(scored, FILL * (half - 1))
                    src = slot_mask[:, ds(half * FILL, FILL), :].rearrange("p u (a t) -> p u a t", a=1)
                    act.copy(mask_rows[:, slot:slot + FILL, :, :],
                             src.to_broadcast([P, FILL, H, UT])).then_inc(mask_rows_ready, 1)

                def copy_k(s, v):
                    u = s * US + v
                    act.wait_ge(k_turned, u + 1)
                    if not (is_first(s) and v < RING):
                        act.wait_ge(scored, u - RING + 1)
                    act.copy(k_t[:, v % RING, :, :].rearrange("p k n -> p (k n)"), k_ps[:, 0:D]).then_inc(k_copied, 1)

                def exponential(s, v):
                    u, h = s * US + v, v % US
                    act.wait_ge(neg_done, u + 1)
                    if not (is_first(s) and v < RING):
                        act.wait_ge(p_turned, u - RING + 1)
                    act.activation(prob[:, v % RING, :], s_ps[v % RING][:, 0:P], ACT.Exp, bias=neg_max[:, h:h + 1], scale=1.0,
                                   accum_out=row_sum[:, h:h + 1]).then_inc(exp_done, 1)

                def keep_context(t, slot):
                    act.wait_ge(weighed, UPT * (t + 1))
                    act.copy(q_t[:, :, ds(t * P, P)], o_ps[slot][:, 0:D].rearrange("p (k n) -> p k n", k=DK)).then_inc(
                        o_copied, 1)

                def sparse(s):
                    for h in range(US):
                        if not (ends(s) and h + 2 >= US):
                            exponential(s + (h + 2) // US, (h + 2) % US)
                        if not (ends(s) and h + 4 >= US):
                            copy_k(s + (h + 4) // US, (h + 4) % US)
                        if h % FILL == 2:
                            n = h // FILL + 2
                            if not (ends(s) and n >= US // FILL):
                                spread_mask(US // FILL * s + n, n % 2 * FILL, False)
                        if h == UPT + 2:
                            keep_context(2 * s, 0)
                        if h == 2 and not is_first(s):
                            keep_context(2 * s - 1, 1)

                act.wait_ge(picks_ready, 1)
                for n in range(2):
                    spread_mask(n, n * FILL, True)
                for v in range(3):
                    copy_k(0, v)
                exponential(0, 0)
                copy_k(0, 3)
                exponential(0, 1)
                steps_loop(act, sparse)
                keep_context(TILES - 1, 1)
                act.wait_ge(o_copied, TILES)
                act.sem_inc(path_done, 1)
            with act.Else():
                act.wait_ge(picks_ready, 1)
                for t in range(TILES):
                    for k in range(DK):
                        act.wait_ge(kt_turned, t * DK + k + 1)
                        act.copy(kt_all[:, k, t * P:(t + 1) * P], banks[k][:, 0:P]).then_inc(kt_copied, 1)

                def exponential(t, h, first):
                    act.wait_ge(negmax_ready, t * H + h + 1)
                    if not first and h % HPG == 0:
                        act.wait_ge(ctx_ready, GROUPS * (t - 1) + h // HPG + 1)
                    act.activation(logits[:, h % LR, :], logits[:, h % LR, :], ACT.Exp, bias=negmax[:, h:h + 1], scale=1.0,
                                   accum_out=sums[:, h:h + 1]).then_inc(probs_ready, 1)

                def copy_quarter(t, h, q, free):
                    u = t * H + h
                    act.wait_ge(quarter_turned, QUARTERS * u + q + 1)
                    if q == 0 and not free:
                        act.wait_ge(ctx_done, u - 1)
                    act.copy(probs_t[:, h % 2, 4 * q:4 * q + 4, :].rearrange("p a b -> p (a b)"),
                             turned[q % 2][:, :]).then_inc(copied_act, 1)

                def copy_ctx(n, units, first):
                    act.wait_ge(ctx_done, units)
                    if not first:
                        act.wait_ge(ctx_back, n)
                    act.copy(ctx_part[:, :], ctx_ps[:, :]).then_inc(ctx_copied, 1)

                def attend(t):
                    first = isinstance(t, int) and t == 0
                    last = isinstance(t, int) and t == TILES - 1
                    for h in range(H):
                        copy_quarter(t, h, 0, first and h < 2)
                        if not (last and h + 1 == H):
                            exponential(t + (h + 1) // H, (h + 1) % H, first and h + 1 < H)
                        copy_quarter(t, h, 2, True)
                        if h == 4:
                            copy_ctx(GROUPS * t, t * H + HPG, first)
                        if h == 0 and not first:
                            copy_ctx(GROUPS * t - 1, t * H, False)

                exponential(0, 0, True)
                attend(0)
                with act.Fori(1, TILES - 1) as t:
                    attend(t)
                attend(TILES - 1)
                copy_ctx(GROUPS * TILES - 1, DENSE_UNITS, False)
                for t in range(TILES):
                    for k in range(DK):
                        act.wait_ge(ctxt_back, t * DK + k + 1)
                        act.copy(q_t[:, k, t * P:(t + 1) * P], banks[k][:, 0:P]).then_inc(ctxt_kept, 1)
                act.wait_ge(ctxt_kept, DK * TILES)
                act.sem_inc(path_done, 1)

            act.wait_ge(path_done, ENGINES)

            def copy_ctxt(t):
                if not is_first(t):
                    act.wait_ge(attn_ready, t)
                act.copy(ctx_t, q_t[:, :, ds(t * P, P)]).then_inc(ctxt_copied, 1)

            def copy_h2(t, r, free):
                act.wait_ge(h2_turned, t + 1)
                if not free:
                    act.wait_ge(hidden_ready, 2 * (t - 1))
                act.copy(h2_t[:, r % 2, :, :], ctx_ps[:, 0:D].rearrange("p (k n) -> p k n", k=DK)).then_inc(h2_copied, 1)

            def gelu(t, half):
                act.wait_ge(hidden_ready, 2 * t + half + 1)
                if not is_first(t):
                    act.wait_ge(ff_ready, t)
                act.activation(gelu_t[:, 4 * half:4 * half + 4, :].rearrange("p a b -> p (a b)"),
                               score[0][:, half * CH:(half + 1) * CH], ACT.Gelu_apprx_tanh).then_inc(gelu_ready, 1)

            copy_ctxt(0)
            copy_ctxt(1)
            copy_h2(0, 0, True)

            def finish(i, last):
                for r in range(FR):
                    t = FR * i + r
                    gelu(t, 0)
                    gelu(t, 1)
                    if not (last and r + 2 >= FR):
                        copy_ctxt(t + 2)
                    if not (last and r + 1 >= FR):
                        copy_h2(t + 1, r + 1, is_first(t))

            finish(0, False)
            with act.Fori(1, TILES // FR - 1) as i:
                finish(i, False)
            finish(TILES // FR - 1, True)


        @block.vector
        def _(dve):
            dve.wait_ge(ident_ready, 1)
            dve.tensor_copy(ident_bf[:, :], ident[:, :]).then_inc(small_step, 1)
            dve.tensor_reduce(quadrant[:, :], ident[:, :].rearrange("p (h t) -> p h t", h=HPG), AX.X,
                              ALU.add).then_inc(small_step, 1)

            def ln1_stats(c, s):
                base = 2 * CT * (2 * c + s)
                dve.wait_ge(x_loaded[s][c % 2], 16 * (c // 2 + 1))
                for i in range(CT):
                    dve.bn_stats(stats[:, s, i, :], h_tok[:, c % 2, s, i, :]).then_inc(stat_step, 1)
                dve.wait_ge(stat_step, base + CT)
                if c > 0:
                    dve.wait_ge(ln1_done, CT * (2 * c + s - 1))
                for i in range(CT):
                    dve.bn_aggr(moments[:, s, i, :], stats[:, s, i, :]).then_inc(stat_step, 1)
                dve.wait_ge(stat_step, base + 2 * CT)
                dve.tensor_scalar(var_eps[:, s, :], moments[:, s, :, 1], EPS, None, ALU.add).then_inc(var_ready, 1)

            def ln1_centre(c, s):
                dve.wait_ge(rstd_ready, 2 * c + s + 1)
                for i in range(CT):
                    row = h_tok[:, c % 2, s, i, :]
                    dve.tensor_scalar(row, row, moments[:, s, i, 0:1], rstd[:, s, i:i + 1], ALU.subtract,
                                      ALU.mult).then_inc(ln1_done, 1)

            def find_edges(t):
                dve.wait_ge(adj_loaded[t % 2], 16 * (t // 2 + 1))
                dve.tensor_scalar(edges[:, t, :], adj_sb[:, t % 2, :], 0.0, None, ALU.not_equal).then_inc(edges_ready, 1)

            def add_kv_bias(t):
                dve.wait_ge(kv_projected, t + 1)
                if t >= CT:
                    dve.wait_ge(mean_summed, t - CT + 1)
                    dve.wait_ge(kv_saved[t % CT], 16 * (t // CT))
                dve.scalar_tensor_tensor(out=kv_out[:, t % CT, :], in0=banks[4 + t % 2], scalar=node[:, t:t + 1],
                                         in1=bkv_bc, op0=ALU.mult, op1=ALU.add).then_inc(kv_ready, 1)

            dve.wait_ge(iota_ready, 1)
            dve.tensor_copy(iota[:, :], keys_iota).then_inc(node_ready, 1)
            for s in range(2):
                ln1_stats(0, s)
            for s in range(2):
                ln1_centre(0, s)
            for t in range(2):
                find_edges(t)
            dve.wait_ge(ln_loaded, 16 * N_LN)
            dve.tensor_scalar(node[:, :], node_i[:, :], 1.0, None, ALU.is_equal).then_inc(node_ready, 1)
            dve.wait_ge(weights_loaded, 16 * N_WEIGHTS)
            dve.tensor_scalar(bq_scaled, bq_col, Q_SCALE, None, ALU.mult).then_inc(node_ready, 1)
            dve.wait_ge(node_ready, 3)
            for c in range(CHUNKS):
                more = c + 1 < CHUNKS
                if more:
                    for s in range(2):
                        ln1_stats(c + 1, s)
                for i in range(2):
                    add_kv_bias(CT * c + i)
                for i in range(2, CT):
                    find_edges(CT * c + i)
                if more:
                    for s in range(2):
                        ln1_centre(c + 1, s)
                for i in range(2, CT):
                    add_kv_bias(CT * c + i)
                if more:
                    for i in range(2):
                        find_edges(CT * (c + 1) + i)
            dve.wait_ge(mean_summed, TILES)
            dve.tensor_copy(mean_v[:, :], banks[7][:, 0:D]).then_inc(mean_ready, 1)

            step = 0

            def picked(ins):
                nonlocal step
                step += 1
                return ins.then_inc(pick_step, 1)

            dve.wait_ge(h_turned, 2 * CHUNKS)
            dve.wait_ge(ht_saved, 16 * CHUNKS)
            for g in range(2):
                for n in range(CODE_BANKS):
                    dve.wait_ge(coded, CODE_BANKS * g + n + 1)
                    dve.scalar_tensor_tensor(out=keys[:, g, n * CH:(n + 1) * CH], in0=banks[n],
                                             scalar=float(N), in1=iota[:, n * CH:(n + 1) * CH], op0=ALU.mult,
                                             op1=ALU.add).then_inc(keys_ready, 1)
                dve.wait_ge(keys_ready, CODE_BANKS * (g + 1))
                for r in range(SEG_PICKS // 8):
                    top = [cand[:, g, n, 8 * r:8 * r + 8] for n in range(SEGS)]
                    seg = [keys[:, g, n * SEG:(n + 1) * SEG] for n in range(SEGS)]
                    for n in range(SEGS):
                        picked(dve.max(top[n], seg[n]))
                    dve.wait_ge(pick_step, step)
                    if 8 * (r + 1) < SEG_PICKS:
                        for n in range(SEGS):
                            picked(dve.match_replace(seg[n], top[n], seg[n], -1.0))
                        dve.wait_ge(pick_step, step)
                picked(dve.tensor_copy(spill[:, g, 0:SEGS], cand[:, g, :, SEG_PICKS - 1]))
                dve.wait_ge(pick_step, step)
            flat = [cand[:, g, :, :].rearrange("p a b -> p (a b)") for g in range(2)]
            for r in range(SLOTS // 8):
                top = [picks[:, g, 8 * r:8 * r + 8] for g in range(2)]
                for g in range(2):
                    if r > 0:
                        dve.wait_ge(pick_step, step - 1)
                    picked(dve.max(top[g], flat[g]))
                if r + 1 < SLOTS // 8:
                    for g in range(2):
                        dve.wait_ge(pick_step, step - 1)
                        picked(dve.match_replace(flat[g], top[g], flat[g], -1.0))
            dve.wait_ge(pick_step, step)
            for g in range(2):
                picked(dve.tensor_copy(spill[:, g, SEGS:SEGS + 1], picks[:, g, SLOTS - 1:SLOTS]))
            dve.wait_ge(pick_step, step)
            picked(dve.tensor_reduce(spill_max[:, :], spill[:, :, :], AX.XY, ALU.max))
            assert step == SPILL_STEP
            dve.wait_ge(spill_turned, 1)
            picked(dve.tensor_reduce(spill_all[:, :], banks[2][0:1, 0:P], AX.X, ALU.max))
            dve.wait_ge(pick_step, step)
            dve.tensor_scalar(dense_flag[:, :], spill_all[:, :], float(N), None, ALU.is_ge).then_inc(flag_ready, 1)

            dve.wait_ge(mean_projected, 1)
            picked(dve.tensor_copy(mean_out[:, :], banks[5][:, 0:D]))

            dve.wait_ge(picks_turned, 1)
            picked(dve.tensor_copy(picks_t[:, :], banks[3][:, 0:P]))
            dve.wait_ge(pick_step, step)
            picked(dve.tensor_scalar(source[:, :], picks_t[:, :], N - 1, None, ALU.bitwise_and))
            picked(dve.tensor_scalar(code[:, :], picks_t[:, :], N.bit_length() - 1, None, ALU.logical_shift_right))
            dve.wait_ge(pick_step, step)
            for b in range(G):
                picked(dve.tensor_scalar(bits[:, b, :], code[:, :], b, 1, ALU.logical_shift_right, ALU.bitwise_and))
            dve.wait_ge(pick_step, step)
            dve.wait_ge(mask_cleared, 1)
            for g in range(2):
                rows = slice(SLOTS * g, SLOTS * (g + 1))
                picked(dve.tensor_scalar(slot_mask[rows, :, G * g:G * (g + 1)], bits[rows, :, :].rearrange("p b u -> p u b"),
                                         -NEG, NEG, ALU.mult, ALU.add))
            dve.wait_ge(degree_ready, TILES)
            picked(dve.tensor_scalar(empty[:, :], degree[:, :], 0.0, None, ALU.is_equal))
            dve.wait_ge(pick_step, step)
            dve.sem_inc(picks_ready, 1)

            flag = read_flag(dve)
            with dve.If(flag == 0):
                def row_maximum(s, v):
                    u, h = s * US + v, v % US
                    dve.wait_ge(scored, u + 1)
                    dve.tensor_reduce(row_max[:, h:h + 1], s_ps[v % RING][:, 0:P], AX.X, ALU.max).then_inc(max_done, 1)

                def negate_maximum(s, v):
                    u, h = s * US + v, v % US
                    dve.wait_ge(max_done, u + 1)
                    dve.tensor_scalar(neg_max[:, h:h + 1], row_max[:, h:h + 1], NO_EDGE, -1.0, ALU.max,
                                      ALU.mult).then_inc(neg_done, 1)

                def fill_q(half, slot, first):
                    if not first:
                        dve.wait_ge(scored, FILL * (half - 1))
                    for k in range(DK):
                        q_units = q_t[:, k, ds(half * FILL * UT, FILL * UT)].rearrange("p (u a t) -> p u a t", u=FILL, a=1)
                        dve.tensor_tensor(
                            q_blocks[:, k, slot:slot + FILL, :].rearrange("p u (q t) -> p u q t", q=HPG),
                            q_units.to_broadcast([P, FILL, HPG, UT]),
                            quadrant[:, :].rearrange("p (a q b) -> p a q b", a=1, b=1).to_broadcast([P, FILL, HPG, UT]),
                            ALU.mult).then_inc(q_blocks_ready, 1)

                def copy_p(s, v):
                    u = s * US + v
                    dve.wait_ge(p_turned, u + 1)
                    if not (is_first(s) and v < RING):
                        dve.wait_ge(weighed, u - RING + 1)
                    dve.tensor_copy(prob_t[:, v % RING, :], p_ps[:, 0:P]).then_inc(p_copied, 1)

                def normalise(s, v, between):
                    u, h = s * US + v, v % US
                    dve.wait_ge(exp_done, u + 1)
                    dve.tensor_scalar(row_sum_up[:, h:h + 1], row_sum[:, h:h + 1], TINY, None, ALU.max).then_inc(
                        norm_step, 1)
                    between[0]()
                    dve.wait_ge(norm_step, 3 * u + 1)
                    dve.reciprocal(row_recip[:, h:h + 1], row_sum_up[:, h:h + 1]).then_inc(norm_step, 1)
                    between[1]()
                    dve.wait_ge(norm_step, 3 * u + 2)
                    dve.tensor_scalar(prob[:, v % RING, :], prob[:, v % RING, :], row_recip[:, h:h + 1], None,
                                      ALU.mult).then_inc(norm_step, 1)

                def nothing():
                    pass

                def sparse(s):
                    for h in range(US):
                        between = [nothing, nothing]
                        if not (ends(s) and h + 2 >= US):
                            ahead = s + (h + 2) // US, (h + 2) % US
                            between = [lambda: row_maximum(*ahead), lambda: negate_maximum(*ahead)]
                        if not (ends(s) and h + 1 >= US):
                            normalise(s + (h + 1) // US, (h + 1) % US, between)
                        copy_p(s, h)
                        if h % FILL == 2:
                            n = h // FILL + 2
                            if not (ends(s) and n >= US // FILL):
                                fill_q(US // FILL * s + n, n % 2 * FILL, False)

                dve.wait_ge(small_step, 2)
                dve.wait_ge(q_copied, DK * CHUNKS)
                for n in range(2):
                    fill_q(n, n * FILL, True)
                row_maximum(0, 0)
                negate_maximum(0, 0)
                normalise(0, 0, [lambda: row_maximum(0, 1), lambda: negate_maximum(0, 1)])
                steps_loop(dve, sparse)
                dve.wait_ge(p_copied, UNITS)
                dve.sem_inc(path_done, 1)
            with dve.Else():
                def make_mask(t, first):
                    dve.wait_ge(adj_again, 16 * (t + 1))
                    if not first:
                        dve.wait_ge(masked, 2 * t * H)
                    dve.tensor_scalar(mask_sb[:, :], adj_sb[:, 0, :], 0.0, NEG, ALU.is_equal, ALU.mult).then_inc(mask_ready, 1)
                    dve.wait_ge(mask_ready, t + 1)

                def mask_half(t, h, half, free):
                    u = t * H + h
                    if half == 0 and not free:
                        dve.wait_ge(quarter_turned, QUARTERS * (u - LR + 1))
                    if half == 1:
                        dve.wait_ge(masked, 2 * u + 1)
                    wait_alone(dve, scores_ready, 2 * u + half + 1)
                    start = LOWEST if half == 0 else rowmax[:, h, 0:1]
                    dve.tensor_tensor_reduce(logits[:, h % LR, half * HALF:(half + 1) * HALF], score[half][:, :],
                                             mask_sb[:, half * HALF:(half + 1) * HALF], 1.0, start, ALU.add, ALU.max,
                                             rowmax[:, h, half:half + 1]).then_inc(masked, 1)

                def negate(t, h):
                    dve.wait_ge(masked, 2 * (t * H + h) + 2)
                    dve.tensor_scalar(negmax[:, h:h + 1], rowmax[:, h, 1:2], -1.0, None, ALU.mult).then_inc(negmax_ready, 1)

                def copy_quarter(t, h, q, free):
                    u = t * H + h
                    dve.wait_ge(quarter_turned, QUARTERS * u + q + 1)
                    if q == 1 and not free:
                        dve.wait_ge(ctx_done, u - 1)
                    dve.tensor_copy(probs_t[:, h % 2, 4 * q:4 * q + 4, :].rearrange("p a b -> p (a b)"),
                                    turned[q % 2][:, :]).then_inc(copied_dve, 1)

                def normalise(n, g, saved):
                    if saved is not None:
                        dve.wait_ge(ctx_saved, saved)
                    dve.wait_ge(ctx_back, n + 1)
                    dve.tensor_reduce(ctx_sum[:, :, :], back_ps[:, :].rearrange("p (h j d) -> p h d j", h=HPG, j=HPG), AX.X,
                                      ALU.add).then_inc(ctx_step, 1)
                    dve.reciprocal(recip[:, :], sums[:, g * HPG:(g + 1) * HPG]).then_inc(ctx_step, 1)
                    dve.wait_ge(ctx_step, 2 * n + 2)
                    for i in range(HPG):
                        last = dve.tensor_scalar(ctx_norm[:, (g * HPG + i) * HD:(g * HPG + i + 1) * HD], ctx_sum[:, i, :],
                                                 recip[:, i:i + 1], None, ALU.mult)
                    last.then_inc(ctx_ready, 1)

                def attend(t):
                    first = isinstance(t, int) and t == 0
                    last = isinstance(t, int) and t == TILES - 1
                    for h in range(H):
                        hm, tm = (h + 2) % H, t + (h + 2) // H
                        more = not (last and h + 2 >= H)
                        free = first and h + 2 < LR
                        if more:
                            if hm == 0:
                                make_mask(tm, False)
                            mask_half(tm, hm, 0, free)
                        copy_quarter(t, h, 1, first and h < 2)
                        if more:
                            mask_half(tm, hm, 1, free)
                            negate(tm, hm)
                        copy_quarter(t, h, 3, True)
                        if h == 5:
                            normalise(GROUPS * t, 0, None if first else 16 * t)
                        if h == 1 and not first:
                            normalise(GROUPS * t - 1, 1, None)

                make_mask(0, True)
                for h in range(2):
                    for half in range(2):
                        mask_half(0, h, half, True)
                    negate(0, h)
                attend(0)
                with dve.Fori(1, TILES - 1) as t:
                    attend(t)
                attend(TILES - 1)
                normalise(GROUPS * TILES - 1, 1, None)
                dve.wait_ge(ctx_ready, GROUPS * TILES)
                dve.memset(empty[:, :], 0.0).then_inc(empty_ready, 1)
                dve.wait_ge(empty_ready, 1)
                dve.sem_inc(path_done, 1)

            dve.wait_ge(path_done, ENGINES)
            dve.wait_ge(weights3_loaded, 16 * N_WEIGHTS3)

            def make_bias(t, r):
                dve.scalar_tensor_tensor(out=bias_row[:, r % 2, :], in0=mean_out[:, :], scalar=empty[:, ds(t, 1)],
                                         in1=bo_bc, op0=ALU.mult, op1=ALU.add).then_inc(bias_ready, 1)

            def row_stats(src, slot, step, base):
                dve.wait_ge(step, base)
                dve.bn_stats(stats[:, slot, 0, :], src).then_inc(step, 1)
                wait_alone(dve, step, base + 1)
                dve.bn_aggr(moments[:, slot, 0, :], stats[:, slot, 0, :]).then_inc(step, 1)
                dve.wait_ge(step, base + 2)
                dve.tensor_scalar(var_eps[:, slot, 0:1], moments[:, slot, 0, 1:2], EPS, None, ALU.add).then_inc(step, 1)

            def ln2_sum(t, r, i):
                base = 8 * t
                dve.wait_ge(attn_ready, t + 1)
                if not is_first(t):
                    dve.wait_ge(ln2_step, base)
                dve.wait_ge(bias_ready, t + 1)
                dve.tensor_tensor(res, turned[1][:, 0:D], bias_row[:, r % 2, :], ALU.add).then_inc(ln2_step, 1)
                dve.wait_ge(ln2_step, base + 1)
                dve.wait_ge(rows_loaded[r % FR], 32 * (i + 1 + r // FR))
                dve.scalar_tensor_tensor(out=res, in0=res, scalar=node[:, ds(t, 1)], in1=rows_in[:, r % FR, 0, :],
                                         op0=ALU.mult, op1=ALU.add).then_inc(ln2_step, 1)
                row_stats(res, 0, ln2_step, base + 2)

            def ln2_scale(t, r):
                base = 8 * t
                m = node[:, ds(t, 1)]
                dve.wait_ge(rstd2_ready, t + 1)
                dve.tensor_scalar(res, res, moments[:, 0, 0, 0:1], rstd[:, 0, 0:1], ALU.subtract,
                                  ALU.mult).then_inc(ln2_step, 1)
                dve.wait_ge(ln2_step, base + 6)
                dve.scalar_tensor_tensor(out=res, in0=res, scalar=m, in1=scale2_bc, op0=ALU.mult,
                                         op1=ALU.mult).then_inc(ln2_step, 1)
                dve.wait_ge(ln2_step, base + 7)
                dve.scalar_tensor_tensor(out=h2[:, r % 2, :], in0=bias2_bc, scalar=m, in1=res, op0=ALU.mult,
                                         op1=ALU.add).then_inc(ln2_step, 1)

            def ln3_sum(t, r):
                base = 6 * t
                dve.wait_ge(ff_ready, t + 1)
                if not is_first(t):
                    dve.wait_ge(ln3_step, base)
                dve.tensor_tensor(res2, back_ps[:, 0:D], h2[:, r % 2, :], ALU.add).then_inc(ln3_step, 1)
                dve.wait_ge(ln3_step, base + 1)
                dve.tensor_tensor(res2, res2, rows_in[:, r % FR, 1, :], ALU.add).then_inc(ln3_step, 1)
                row_stats(res2, 1, ln3_step, base + 2)

            def ln3_scale(t, r, i):
                dve.wait_ge(rstd3_ready, t + 1)
                if not (isinstance(i, int) and i == 0 and r < 2):
                    dve.wait_ge(y_saved[r % 2], 16 * (FR // 2 * i + r // 2))
                dve.tensor_scalar(y_out[:, r % 2, :], res2, moments[:, 1, 0, 0:1], rstd[:, 1, 0:1], ALU.subtract,
                                  ALU.mult).then_inc(ln3_step, 1)

            for t in range(2):
                make_bias(t, t)
            for t in range(2):
                ln2_sum(t, t, 0)
                ln2_scale(t, t)
            make_bias(2, 2)

            def finish(i, last):
                for r in range(FR):
                    t = FR * i + r
                    if not (last and r + 2 >= FR):
                        ln2_sum(t + 2, r + 2, i)
                    ln3_sum(t, r)
                    if not (last and r + 2 >= FR):
                        ln2_scale(t + 2, r + 2)
                    if not (last and r + 3 >= FR):
                        make_bias(t + 3, r + 3)
                    ln3_scale(t, r, i)

            finish(0, False)
            with dve.Fori(1, TILES // FR - 1) as i:
                finish(i, False)
            finish(TILES // FR - 1, True)


_INS = ["x", "adj", "nodemask", "L0_gnn_h_target", "L0_gnn_ln1_scale", "L0_gnn_ln1_bias", "L0_gnn_Wq", "L0_gnn_bq",
        "L0_gnn_Wk", "L0_gnn_bk", "L0_gnn_Wv", "L0_gnn_bv", "L0_gnn_Wo", "L0_gnn_bo", "L0_gnn_ln2_scale",
        "L0_gnn_ln2_bias", "L0_gnn_W1", "L0_gnn_W2"]


def kernel(**inputs):
    import numpy as _np
    import concourse.bacc as _bacc
    from concourse import mybir as _mybir
    from concourse.bass_utils import run_bass_kernel_spmd as _run

    nc = _bacc.Bacc("TRN2", target_bir_lowering=False, num_devices=1)
    arrays, args = {}, []
    for name in _INS:
        a = _np.ascontiguousarray(inputs[name])
        arrays[f"in_{name}_dram"] = a
        args.append(nc.dram_tensor(f"in_{name}_dram", a.shape, _mybir.dt.from_np(a.dtype), kind="ExternalInput").ap())
    shape = inputs["x"].shape
    args.append(nc.dram_tensor("out_0_dram", shape, _mybir.dt.float32, kind="ExternalOutput").ap())
    graph_attention(nc, *args)
    r = _run(nc, [arrays], core_ids=[0])
    return r.results[0]["out_0_dram"]
```
